# Optimizing a Trainium2 kernel written in Bass

```python
import numpy as np
import jax
import jax.numpy as jnp

def _softmax(x, axis=-1):
    return jax.nn.softmax(x, axis=axis)

def _gelu(x):
    return jax.nn.gelu(x, approximate=True)

def _silu(x):
    return jax.nn.silu(x)

def _sigmoid(x):
    return jax.nn.sigmoid(x)

def _layernorm(x, axis=-1, eps=1e-05):
    m = jnp.mean(x, axis=axis, keepdims=True)
    v = jnp.var(x, axis=axis, keepdims=True)
    return (x - m) / jnp.sqrt(v + eps)

def _scatter_add(tgt, idx, src, axis=0):
    return tgt.at[idx].add(src)

def _segment_sum(src, seg, n):
    return jax.ops.segment_sum(src, seg, n)
kernel_name = 'mk_prb_d1_jaxref_r8_60bc6a'

def setup_inputs(seed: int=0):
    np.random.seed(seed)
    _w = jnp.asarray

    def _L0_attn_setup():
        import jax, jax.numpy as jnp
        import numpy as np
        H = 16
        D = 128
        key = jax.random.key(seed)
        k1, k2, k3 = jax.random.split(key, 3)
        B, S, dim = (2, 256, 256)
        x = jax.random.normal(k1, (B, S, dim), dtype=jnp.float32)
        Wqkv = jax.random.normal(k2, ((H + 2 * H) * D, dim), dtype=jnp.float32) * 0.02
        Wout = jax.random.normal(k3, (dim, H * D), dtype=jnp.float32) * 0.02
        return {'x': x, 'Wqkv': Wqkv, 'Wout': Wout}
    _L0_attn_in = _L0_attn_setup()

    def _L0_ffn_setup():
        import jax, jax.numpy as jnp
        import numpy as np
        EPS = 1e-08

        def _quantize(w):
            gamma = jnp.mean(jnp.abs(w))
            return jnp.clip(jnp.round(w / (gamma + EPS)), -1.0, 1.0)

        def _bitlinear(x, w):
            return jnp.matmul(x, _quantize(w).T)
        key = jax.random.key(seed)
        k1, k2, k3, k4 = jax.random.split(key, 4)
        d, h = (256, 704)
        x = jax.random.normal(k1, (4, 256, d), dtype=jnp.float32)
        w1 = jax.random.normal(k2, (h, d), dtype=jnp.float32)
        w2 = jax.random.normal(k3, (h, d), dtype=jnp.float32)
        w3 = jax.random.normal(k4, (d, h), dtype=jnp.float32)
        return {'x': x, 'w1': w1, 'w2': w2, 'w3': w3}
    _L0_ffn_in = _L0_ffn_setup()
    _d = {'L0_attn_x': _L0_attn_in['x'], 'L0_attn_Wqkv': _L0_attn_in['Wqkv'], 'L0_attn_Wout': _L0_attn_in['Wout'], 'L0_ffn_w1': _L0_ffn_in['w1'], 'L0_ffn_w2': _L0_ffn_in['w2'], 'L0_ffn_w3': _L0_ffn_in['w3']}
    _x0 = _d['L0_attn_x']
    _d['L0_attn_x'] = jax.random.normal(jax.random.fold_in(jax.random.key(seed), 1), (1, 2048, 256), dtype=_x0.dtype)
    del _x0
    return _d

def reference(L0_attn_x, L0_attn_Wqkv, L0_attn_Wout, L0_ffn_w1, L0_ffn_w2, L0_ffn_w3):

    def _L0_attn_ref(x, Wqkv, Wout):
        import jax, jax.numpy as jnp
        import numpy as np
        H = 16
        D = 128
        B, S, _ = x.shape
        qkv = jnp.einsum('bsd,ed->bse', x, Wqkv)
        qkv = qkv.reshape(B, S, 3 * H, D)
        q = qkv[:, :, :H]
        k = qkv[:, :, H:2 * H]
        v = qkv[:, :, 2 * H:]
        logits = jnp.einsum('bqhd,bkhd->bhqk', q, k) * D ** (-0.5)
        w = jax.nn.softmax(logits.astype(jnp.float32), axis=-1).astype(logits.dtype)
        out = jnp.einsum('bhqk,bkhd->bqhd', w, v).reshape(B, S, H * D)
        return jnp.einsum('bse,de->bsd', out, Wout)

    def _L0_ffn_ref(x, w1, w2, w3):
        import jax, jax.numpy as jnp
        import numpy as np
        EPS = 1e-08

        def _quantize(w):
            gamma = jnp.mean(jnp.abs(w))
            return jnp.clip(jnp.round(w / (gamma + EPS)), -1.0, 1.0)

        def _bitlinear(x, w):
            return jnp.matmul(x, _quantize(w).T)
        x1 = _bitlinear(x, w1)
        x2 = _bitlinear(x, w2)
        hidden = jax.nn.sigmoid(x1) * x2
        return _bitlinear(hidden, w3)
    x = L0_attn_x
    xn = _layernorm(x, axis=-1)
    x = x + _L0_attn_ref(xn, L0_attn_Wqkv, L0_attn_Wout) + _L0_ffn_ref(xn, L0_ffn_w1, L0_ffn_w2, L0_ffn_w3)
    return x

_drawn_inputs = setup_inputs


def setup_inputs(seed=0):
    import zlib

    import numpy as np

    out = dict(_drawn_inputs(seed))
    spreads = {}
    factors = {'L0_attn_Wqkv': 8.0, 'L0_attn_Wout': 8.0}
    for name, (base, spread) in spreads.items():
        noise = np.random.default_rng([zlib.crc32(name.encode()), seed]).standard_normal(out[name].shape)
        drawn = base * np.exp(spread * noise) if base else spread * noise
        out[name] = jnp.asarray(drawn.astype(out[name].dtype))
    for name, factor in factors.items():
        out[name] = (out[name] * factor).astype(out[name].dtype)
    return out
```

```python
import concourse.bass as bass
from concourse import mybir
from contextlib import ExitStack

F32 = mybir.dt.float32
F32R = mybir.dt.float32r
ALU = mybir.AluOpType
ACT = mybir.ActivationFunctionType
AX_X = mybir.AxisListType.X

P = 128
S = 2048
DIM = 256
H = 16
D = 128
FF = 704
C = DIM // P
T = S // P
PAIRS = T // 2
FB = -(-FF // P)
FR = FF - (FB - 1) * P
G = 4
CH = S // G
TG = CH // P
HALF = S // 2
KH = HALF // P
SCALE = float(D) ** -0.5
LN_EPS = 1e-5
Q_EPS = 1e-8

SCORES = EXPS = TRANS = PT = 2 * T
PROJ = 4
VALS = 4
YACC = T
LN_STEPS = 9


def build(nc, x_d, wqkv_d, wo_d, w1_d, w2_d, w3_d, out_d):
    ctx = ExitStack()
    with ctx:
        def sb(name, shape, dt=F32, where=ctx):
            return where.enter_context(nc.sbuf_tensor(name, shape, dt))

        def sem(name):
            return ctx.enter_context(nc.semaphore(name))

        y = sb("y", [P, T, DIM])
        xt_hi = sb("xt_hi", [P, C, S], F32R)
        xt_lo = sb("xt_lo", [P, C, S], F32R)
        k_hi = sb("k_hi", [P, S], F32R)
        k_lo = sb("k_lo", [P, S], F32R)
        q_hi = sb("q_hi", [P, S], F32R)
        q_lo = sb("q_lo", [P, S], F32R)
        v_hi = sb("v_hi", [P, T, D], F32R)
        v_lo = sb("v_lo", [P, T, D], F32R)
        wqkv_raw = sb("wqkv_raw", [P, C, 3 * D])
        wqkv_hi = sb("wqkv_hi", [P, C, 3 * D], F32R)
        wqkv_lo = sb("wqkv_lo", [P, C, 3 * D], F32R)
        wo_raw = sb("wo_raw", [P, DIM])
        wo_hi = sb("wo_hi", [P, DIM], F32R)
        wo_lo = sb("wo_lo", [P, DIM], F32R)
        o_low = sb("o_low", [P, 2 * P])
        o_sum = sb("o_sum", [P, 2 * P])
        o_hi = sb("o_hi", [P, 2 * P], F32R)
        o_lo = sb("o_lo", [P, 2 * P], F32R)
        ident = sb("ident", [P, P])
        zeros = sb("zeros", [P, C, 3 * D])
        row_max = sb("row_max", [P, T, 2])
        neg_max = sb("neg_max", [P, T])
        row_sum = sb("row_sum", [P, T, 2])
        denom = sb("denom", [P, T])
        inv_denom = sb("inv_denom", [P, T])

        with ExitStack() as early:
            w1_raw = sb("w1_raw", [P, C, FF], where=early)
            w2_raw = sb("w2_raw", [P, C, FF], where=early)
            w3_raw = sb("w3_raw", [P, FB, DIM], where=early)
            w1_q = sb("w1_q", [P, C, FB * P], F32R, early)
            w2_q = sb("w2_q", [P, C, FB * P], F32R, early)
            w3_q = sb("w3_q", [P, FB, DIM], F32R, early)
            below = sb("below", [P, FB * DIM], where=early)
            ones = sb("ones", [P, P], where=early)
            abs_sum = sb("abs_sum", [P, 4], where=early)
            abs_tot = sb("abs_tot", [P, 4], where=early)
            gamma = sb("gamma", [P, 3], where=early)
            half_gamma = sb("half_gamma", [P, 2, 3], where=early)
            junk = sb("junk", [P, FB * DIM], where=early)
            stats = sb("stats", [P, TG, 6], where=early)
            mean = sb("mean", [P, TG], where=early)
            diff = sb("diff", [P, TG], where=early)
            var_eps = sb("var_eps", [P, TG], where=early)
            std = sb("std", [P, TG], where=early)
            rstd = sb("rstd", [P, TG], where=early)
            newton = sb("newton", [P, TG], where=early)
            xn = sb("xn", [P, TG, DIM], where=early)
            sig = sb("sig", [P, 2, CH], where=early)
            hid = sb("hid", [P, 2, CH], where=early)
            hid_hi = sb("hid_hi", [P, FB, CH], F32R, early)
            hid_lo = sb("hid_lo", [P, FB, CH], F32R, early)
        prob = sb("prob", [P, 2, S])
        pt = sb("pt", [P, 2, T, 4 * P], F32R)

        ps_s = ctx.enter_context(nc.psum_tensor("ps_s", [P, 4, 512], F32))
        ps_t = ctx.enter_context(nc.psum_tensor("ps_t", [P, 2, 512], F32))
        ps_o = ctx.enter_context(nc.psum_tensor("ps_o", [P, 2, 512], F32))

        s_x = sem("x_loaded")
        s_w = [sem("w1_loaded"), sem("w2_loaded"), sem("w3_loaded")]
        s_wqkv_in = sem("wqkv_loaded")
        s_wo_in = sem("wo_loaded")
        s_const = sem("constants_ready")
        s_pads = sem("pads_zeroed")
        s_abs = sem("abs_sums_ready")
        s_tot = sem("abs_totals_ready")
        s_quant = sem("rounded_signs_ready")
        s_wq = sem("quantised_weights_ready")
        s_ln = sem("layernorm_step_done")
        s_std = sem("std_ready")
        s_xn = sem("normalised_ready")
        s_xtr = sem("normalised_transposed")
        s_xth = sem("xt_high_ready")
        s_xtl = sem("xt_low_ready")
        s_up = sem("ffn_up_done")
        s_sig = sem("sigmoid_ready")
        s_hid = sem("hidden_ready")
        s_hidh = sem("hidden_high_ready")
        s_hidl = sem("hidden_low_ready")
        s_down = sem("ffn_down_done")
        s_wqkv = sem("wqkv_split")
        s_whalf = sem("wqkv_high_ready")
        s_wo = sem("wo_split")
        s_wohalf = sem("wo_high_ready")
        s_proj = sem("keys_queries_done")
        s_projh = sem("keys_queries_high_ready")
        s_projl = sem("keys_queries_low_ready")
        s_val = sem("values_done")
        s_valh = sem("values_high_ready")
        s_vall = sem("values_low_ready")
        s_scores = sem("logits_done")
        s_mx = sem("half_max_ready")
        s_nm = sem("neg_max_ready")
        s_exp = sem("exponentials_ready")
        s_tr = sem("transposes_done")
        s_pth = sem("pt_high_ready")
        s_ptl = sem("pt_low_ready")
        s_pv = sem("values_product_done")
        s_olow = sem("low_output_copied")
        s_osum = sem("output_summed")
        s_ohi = sem("output_high_ready")
        s_osp = sem("output_split")
        s_den = sem("denominator_ready")
        s_inv = sem("inverse_ready")
        s_y = sem("projection_done")
        s_yacc = sem("result_added")
        s_out = sem("result_stored")

        block = ctx.enter_context(nc.Block())

        @block.sync
        def _(sp):
            x_v = x_d.rearrange("(t p) c -> p t c", p=P)
            for g in range(G):
                if g:
                    sp.wait_ge(s_x, 16 * g)
                sp.dma_start(y[:, g * TG:(g + 1) * TG, :], x_v[:, g * TG:(g + 1) * TG, :]).then_inc(s_x, 16)
                if g == 0:
                    sp.dma_start(w1_raw[:], w1_d.rearrange("(c p) f -> p c f", p=P)).then_inc(s_w[0], 16)
                    sp.dma_start(w2_raw[:], w2_d.rearrange("(c p) f -> p c f", p=P)).then_inc(s_w[1], 16)
            sp.dma_start(w3_raw[:, 0:FB - 1, :],
                         w3_d[0:(FB - 1) * P, :].rearrange("(b p) c -> p b c", p=P)).then_inc(s_w[2], 16)
            sp.dma_start(w3_raw[0:FR, FB - 1, :], w3_d[(FB - 1) * P:FF, :]).then_inc(s_w[2], 16)
            sp.dma_start(wqkv_raw[:], wqkv_d[0:1].rearrange("h p c e -> p (h c) e")).then_inc(s_wqkv_in, 16)
            sp.dma_start(wo_raw[:], wo_d[0:1].rearrange("h p c -> p (h c)")).then_inc(s_wo_in, 16)
            with sp.Fori(0, H - 1) as h:
                sp.wait_ge(s_wqkv, h + 1)
                sp.dma_start(wqkv_raw[:],
                             wqkv_d[bass.ds(h + 1, 1)].rearrange("h p c e -> p (h c) e")).then_inc(s_wqkv_in, 16)
                sp.wait_ge(s_wo, h + 1)
                sp.dma_start(wo_raw[:],
                             wo_d[bass.ds(h + 1, 1)].rearrange("h p c -> p (h c)")).then_inc(s_wo_in, 16)
            out_v = out_d.rearrange("(t p) c -> p t c", p=P)
            for p in range(PAIRS):
                sp.wait_ge(s_yacc, YACC * H + 2 * p + 2)
                sp.dma_start(out_v[:, 2 * p:2 * p + 2, :], y[:, 2 * p:2 * p + 2, :]).then_inc(s_out, 16)
            sp.wait_ge(s_out, 16 * PAIRS)

        @block.tensor
        def _(pe):
            def project(first, part, half):
                for bank in (2 * half, 2 * half + 1):
                    col = slice(bank * 512, bank * 512 + 512)
                    n = 0
                    for c in range(C):
                        for w, x in ((wqkv_hi, xt_hi), (wqkv_hi, xt_lo), (wqkv_lo, xt_hi)):
                            last = nc.tensor.matmul(ps_s[:, bank, :], w[:, c, part * D:(part + 1) * D],
                                                    x[:, c, col], start=(n == 0), stop=(n == 3 * C - 1))
                            n += 1
                last.then_inc(s_proj, 1)

            def values(bank, piece):
                for j in range(4):
                    kb = piece * 4 + j
                    n = 0
                    for c in range(C):
                        for x, w in ((xt_hi, wqkv_hi), (xt_hi, wqkv_lo), (xt_lo, wqkv_hi)):
                            last = nc.tensor.matmul(bank[:, j * D:(j + 1) * D], x[:, c, kb * P:(kb + 1) * P],
                                                    w[:, c, 2 * D:3 * D], start=(n == 0), stop=(n == 3 * C - 1))
                            n += 1
                last.then_inc(s_val, 1)

            def logits(t, half):
                for bank in (2 * half, 2 * half + 1):
                    col = slice(bank * 512, bank * 512 + 512)
                    tile = slice(t * P, (t + 1) * P)
                    nc.tensor.matmul(ps_s[:, bank, :], q_hi[:, tile], k_hi[:, col], start=True, stop=False)
                    nc.tensor.matmul(ps_s[:, bank, :], q_hi[:, tile], k_lo[:, col], start=False, stop=False)
                    last = nc.tensor.matmul(ps_s[:, bank, :], q_lo[:, tile], k_hi[:, col], start=False, stop=True)
                last.then_inc(s_scores, 1)

            def transposes(t, half):
                for i in range(KH):
                    kb = half * KH + i
                    last = nc.tensor.transpose(ps_t[:, i // 4, (i % 4) * P:(i % 4 + 1) * P],
                                               prob[:, t % 2, kb * P:(kb + 1) * P], ident[:])
                last.then_inc(s_tr, 1)

            def products(p, half):
                for i in range(KH):
                    kb = half * KH + i
                    nc.tensor.matmul(ps_o[:, p % 2, :], v_hi[:, kb, :], pt[:, p % 2, kb, :],
                                     start=(kb == 0), stop=(kb == T - 1), skip_group_check=True)
                    last = nc.tensor.matmul(ps_o[:, p % 2, 0:2 * P], v_lo[:, kb, :], pt[:, p % 2, kb, 0:2 * P],
                                            start=False, stop=(kb == T - 1), skip_group_check=True)
                if half:
                    last.then_inc(s_pv, 1)

            def out_projection(p):
                for j in range(2):
                    tile = slice(j * P, (j + 1) * P)
                    dst = ps_o[:, p % 2, j * DIM:(j + 1) * DIM]
                    nc.tensor.matmul(dst, o_hi[:, tile], wo_hi[:], start=True, stop=False)
                    nc.tensor.matmul(dst, o_hi[:, tile], wo_lo[:], start=False, stop=False)
                    last = nc.tensor.matmul(dst, o_lo[:, tile], wo_hi[:], start=False, stop=True)
                last.then_inc(s_y, 1)

            pe.wait_ge(s_const, 1)
            pe.wait_ge(s_abs, 4)
            nc.tensor.matmul(ps_o[:, 0, 0:4], ones[:], abs_sum[:], start=True, stop=True).then_inc(s_tot, 1)

            with pe.Fori(0, G) as g:
                pe.wait_ge(s_xn, g + 1)
                for c in range(C):
                    for j in range(TG):
                        last = nc.tensor.transpose(ps_t[:, c, j * P:(j + 1) * P],
                                                   xn[:, j, c * P:(c + 1) * P], ident[:])
                last.then_inc(s_xtr, 1)
                pe.wait_ge(s_xtl, C * g + C)
            pe.wait_ge(s_wq, 2)
            with pe.Fori(0, G) as g:
                for b in range(FB):
                    if b >= 2:
                        pe.wait_ge(s_hid, g * FB + b - 1)
                    for w, k in ((w1_q, 0), (w2_q, 1)):
                        n = 0
                        for c in range(C):
                            for x in (xt_hi, xt_lo):
                                last = nc.tensor.matmul(ps_s[:, 2 * (b % 2) + k, :], w[:, c, b * P:(b + 1) * P],
                                                        x[:, c, bass.ds(g * CH, CH)],
                                                        start=(n == 0), stop=(n == 2 * C - 1))
                                n += 1
                    last.then_inc(s_up, 1)
                pe.wait_ge(s_wq, 4)
                for b in range(FB):
                    pe.wait_ge(s_hidl, g * FB + b + 1)
                    for j in range(TG):
                        dst = (ps_t if j < 2 else ps_o)[:, j % 2, 0:DIM]
                        nc.tensor.matmul(dst, hid_hi[:, b, j * P:(j + 1) * P], w3_q[:, b, :],
                                         start=(b == 0), stop=False)
                        last = nc.tensor.matmul(dst, hid_lo[:, b, j * P:(j + 1) * P], w3_q[:, b, :],
                                                start=False, stop=(b == FB - 1))
                last.then_inc(s_down, 1)
                pe.wait_ge(s_yacc, TG * g + TG)
            pe.wait_ge(s_wqkv, 1)
            for part in (1, 0):
                for half in (0, 1):
                    if part == 0:
                        pe.wait_ge(s_projl, half + 1)
                    project(0, part, half)

            def head(h, last_head):
                for t in range(T):
                    for half in (0, 1):
                        if t == 0:
                            pe.wait_ge(s_projl, PROJ * h + 3 + half)
                        else:
                            pe.wait_ge(s_exp, EXPS * h + 2 * (t - 1) + half + 1)
                        logits(t, half)
                    if t == 0:
                        pe.wait_ge(s_wqkv, h + 1)
                        values(ps_t[:, 0, :], 0)
                        values(ps_t[:, 1, :], 1)
                    if t >= 1:
                        if t == 1:
                            pe.wait_ge(s_vall, VALS * h + 2)
                        else:
                            pe.wait_ge(s_ptl, PT * h + 2 * (t - 1))
                        pe.wait_ge(s_exp, EXPS * h + 2 * (t - 1) + 1)
                        transposes(t - 1, 0)
                    if t == 1:
                        pe.wait_ge(s_yacc, YACC * h + 14)
                        values(ps_o[:, 0, :], 2)
                    if t == 2:
                        pe.wait_ge(s_yacc, YACC * h + 16)
                        values(ps_o[:, 1, :], 3)
                    if t >= 3 and t % 2:
                        p = (t - 3) // 2
                        if p == 0:
                            pe.wait_ge(s_vall, VALS * h + 3)
                        if p == 1:
                            pe.wait_ge(s_vall, VALS * h + 4)
                        if p >= 2:
                            pe.wait_ge(s_yacc, YACC * h + 16 + 2 * (p - 1))
                        pe.wait_ge(s_ptl, PT * h + 4 * p + 3)
                        products(p, 0)
                    if t >= 4 and t % 2 == 0:
                        p = (t - 4) // 2
                        if p == 0:
                            pe.wait_ge(s_vall, VALS * h + 4)
                        pe.wait_ge(s_ptl, PT * h + 4 * p + 4)
                        products(p, 1)
                    if t >= 5 and t % 2:
                        p = (t - 5) // 2
                        if p == 0:
                            pe.wait_ge(s_wo, h + 1)
                        pe.wait_ge(s_osp, PAIRS * h + p + 1)
                        out_projection(p)
                    if t >= 1:
                        pe.wait_ge(s_ptl, PT * h + 2 * (t - 1) + 1)
                        pe.wait_ge(s_exp, EXPS * h + 2 * (t - 1) + 2)
                        transposes(t - 1, 1)
                if not last_head:
                    pe.wait_ge(s_wqkv, h + 2)
                    for half in (0, 1):
                        pe.wait_ge(s_exp, EXPS * h + 2 * (T - 1) + half + 1)
                        project(h, 1, half)
                pe.wait_ge(s_ptl, PT * h + 2 * (T - 1))
                pe.wait_ge(s_exp, EXPS * h + 2 * (T - 1) + 1)
                transposes(T - 1, 0)
                pe.wait_ge(s_ptl, PT * h + 4 * 6 + 4)
                products(6, 1)
                pe.wait_ge(s_ptl, PT * h + 2 * (T - 1) + 1)
                pe.wait_ge(s_exp, EXPS * h + 2 * (T - 1) + 2)
                transposes(T - 1, 1)
                pe.wait_ge(s_yacc, YACC * h + 16 + 2 * 6)
                products(7, 0)
                pe.wait_ge(s_osp, PAIRS * h + 7)
                out_projection(6)
                pe.wait_ge(s_ptl, PT * h + 2 * T)
                products(7, 1)
                if not last_head:
                    for half in (0, 1):
                        pe.wait_ge(s_projl, PROJ * (h + 1) + half + 1)
                        project(h, 0, half)
                pe.wait_ge(s_osp, PAIRS * h + 8)
                out_projection(7)

            with pe.Fori(0, H - 1) as h:
                head(h, False)
            head(H - 1, True)

        @block.scalar
        def _(act):
            act.wait_ge(s_const, 1)
            for i, w in enumerate((w1_raw, w2_raw)):
                act.wait_ge(s_w[i], 16)
                if i:
                    act.wait_ge(s_abs, i)
                nc.scalar.activation(junk[:, 0:C * FF], w[:].rearrange("p c f -> p (c f)"), ACT.Abs,
                                     accum_out=abs_sum[:, i:i + 1]).then_inc(s_abs, 1)
            act.wait_ge(s_w[2], 32)
            act.wait_ge(s_abs, 2)
            nc.scalar.activation(junk[:, 0:(FB - 1) * DIM], w3_raw[:, 0:FB - 1, :].rearrange("p b c -> p (b c)"), ACT.Abs,
                                 accum_out=abs_sum[:, 2:3]).then_inc(s_abs, 1)
            act.wait_ge(s_abs, 3)
            nc.scalar.activation(junk[0:FR, 0:DIM], w3_raw[0:FR, FB - 1, :], ACT.Abs,
                                 accum_out=abs_sum[0:FR, 3:4]).then_inc(s_abs, 1)
            with act.Fori(0, G) as g:
                act.wait_ge(s_ln, g * LN_STEPS + 4)
                nc.scalar.activation(std[:], var_eps[:], ACT.Sqrt).then_inc(s_std, 1)
                act.wait_ge(s_xtr, g + 1)
                for c in range(C):
                    nc.scalar.copy(xt_hi[:, c, bass.ds(g * CH, CH)], ps_t[:, c, :]).then_inc(s_xth, 1)
            with act.Fori(0, G) as g:
                for b in range(FB):
                    act.wait_ge(s_up, g * FB + b + 1)
                    if b >= 2:
                        act.wait_ge(s_hid, g * FB + b - 1)
                    nc.scalar.activation(sig[:, b % 2, :], ps_s[:, 2 * (b % 2), :], ACT.Sigmoid).then_inc(s_sig, 1)
                    act.wait_ge(s_hid, g * FB + b + 1)
                    nc.scalar.copy(hid_hi[:, b, :], hid[:, b % 2, :]).then_inc(s_hidh, 1)

            def proj_high(n, dst, half):
                act.wait_ge(s_proj, n)
                nc.scalar.copy(dst[:, half * HALF:(half + 1) * HALF],
                               ps_s[:, 2 * half:2 * half + 2, :].rearrange("p b n -> p (b n)")).then_inc(s_projh, 1)

            def value_high(h, bank, piece):
                act.wait_ge(s_val, VALS * h + piece + 1)
                nc.scalar.copy(v_hi[:, piece * 4:piece * 4 + 4, :].rearrange("p k d -> p (k d)"),
                               bank).then_inc(s_valh, 1)

            def pt_high(h, t, half):
                act.wait_ge(s_tr, TRANS * h + 2 * t + half + 1)
                nc.scalar.copy(pt[:, (t // 2) % 2, half * KH:(half + 1) * KH, (t % 2) * P:(t % 2 + 1) * P],
                               ps_t[:].rearrange("p b (k q) -> p (b k) q", q=P)).then_inc(s_pth, 1)

            def exponential(h, t, half):
                act.wait_ge(s_nm, T * h + t + 1)
                nc.scalar.activation(prob[:, t % 2, half * HALF:(half + 1) * HALF],
                                     ps_s[:, 2 * half:2 * half + 2, :].rearrange("p b n -> p (b n)"), ACT.Exp,
                                     bias=neg_max[:, t:t + 1], scale=SCALE,
                                     accum_out=row_sum[:, t, half:half + 1]).then_inc(s_exp, 1)

            def low_output(h, p):
                act.wait_ge(s_pv, PAIRS * h + p + 1)
                nc.scalar.copy(o_low[:], ps_o[:, p % 2, 2 * P:4 * P]).then_inc(s_olow, 1)

            for half in (0, 1):
                proj_high(half + 1, k_hi, half)
            for half in (0, 1):
                proj_high(half + 3, q_hi, half)

            def head(h, last_head):
                for t in range(T):
                    if t >= 2:
                        pt_high(h, t - 2, 1)
                    if t >= 1:
                        pt_high(h, t - 1, 0)
                    if t == 0:
                        value_high(h, ps_t[:, 0, :], 0)
                    exponential(h, t, 0)
                    exponential(h, t, 1)
                    if t == 0:
                        value_high(h, ps_t[:, 1, :], 1)
                    if t == 1:
                        value_high(h, ps_o[:, 0, :], 2)
                    if t == 2:
                        value_high(h, ps_o[:, 1, :], 3)
                    if t >= 4 and t % 2 == 0:
                        low_output(h, (t - 4) // 2)
                pt_high(h, T - 2, 1)
                if not last_head:
                    for half in (0, 1):
                        proj_high(PROJ * (h + 1) + half + 1, k_hi, half)
                pt_high(h, T - 1, 0)
                low_output(h, 6)
                pt_high(h, T - 1, 1)
                low_output(h, 7)
                if not last_head:
                    for half in (0, 1):
                        proj_high(PROJ * (h + 1) + half + 3, q_hi, half)

            with act.Fori(0, H - 1) as h:
                head(h, False)
            head(H - 1, True)

        @block.vector
        def _(dve):
            with dve.Fori(0, G) as g:
                dve.wait_ge(s_x, 16 * g + 16)
                for j in range(TG):
                    last = nc.vector.bn_stats(stats[:, j, :],
                                              y[:, bass.ds(g * TG + j, 1), :].rearrange("p t c -> p (t c)"))
                last.then_inc(s_ln, 1)
                dve.wait_ge(s_ln, g * LN_STEPS + 1)
                nc.vector.tensor_tensor(mean[:], stats[:, :, 1], stats[:, :, 4], ALU.add)
                nc.vector.tensor_tensor(diff[:], stats[:, :, 1], stats[:, :, 4], ALU.subtract)
                nc.vector.tensor_tensor(var_eps[:], stats[:, :, 2], stats[:, :, 5], ALU.add).then_inc(s_ln, 1)
                dve.wait_ge(s_ln, g * LN_STEPS + 2)
                nc.vector.tensor_scalar(mean[:], mean[:], 0.5, None, ALU.mult)
                nc.vector.tensor_tensor(diff[:], diff[:], diff[:], ALU.mult)
                nc.vector.tensor_scalar(var_eps[:], var_eps[:], 1.0 / DIM, LN_EPS, ALU.mult, ALU.add
                                        ).then_inc(s_ln, 1)
                dve.wait_ge(s_ln, g * LN_STEPS + 3)
                nc.vector.scalar_tensor_tensor(out=var_eps[:], in0=diff[:], scalar=0.25, in1=var_eps[:],
                                               op0=ALU.mult, op1=ALU.add).then_inc(s_ln, 1)
                dve.wait_ge(s_std, g + 1)
                nc.vector.reciprocal(rstd[:], std[:]).then_inc(s_ln, 1)
                dve.wait_ge(s_ln, g * LN_STEPS + 5)
                nc.vector.tensor_tensor(newton[:], rstd[:], rstd[:], ALU.mult).then_inc(s_ln, 1)
                dve.wait_ge(s_ln, g * LN_STEPS + 6)
                nc.vector.tensor_tensor(newton[:], newton[:], var_eps[:], ALU.mult).then_inc(s_ln, 1)
                dve.wait_ge(s_ln, g * LN_STEPS + 7)
                nc.vector.tensor_scalar(newton[:], newton[:], -0.5, 1.5, ALU.mult, ALU.add).then_inc(s_ln, 1)
                dve.wait_ge(s_ln, g * LN_STEPS + 8)
                nc.vector.tensor_tensor(rstd[:], rstd[:], newton[:], ALU.mult).then_inc(s_ln, 1)
                dve.wait_ge(s_ln, g * LN_STEPS + 9)
                for j in range(TG):
                    last = nc.vector.tensor_scalar(xn[:, j, :],
                                                   y[:, bass.ds(g * TG + j, 1), :].rearrange("p t c -> p (t c)"),
                                                   mean[:, j:j + 1], rstd[:, j:j + 1], ALU.subtract, ALU.mult)
                last.then_inc(s_xn, 1)
                for c in range(C):
                    dve.wait_ge(s_xth, C * g + c + 1)
                    nc.vector.tensor_tensor(xt_lo[:, c, bass.ds(g * CH, CH)], ps_t[:, c, :],
                                            xt_hi[:, c, bass.ds(g * CH, CH)], ALU.subtract).then_inc(s_xtl, 1)

            dve.wait_ge(s_tot, 1)
            nc.vector.tensor_copy(abs_tot[:], ps_o[:, 0, 0:4]).then_inc(s_quant, 1)
            dve.wait_ge(s_quant, 1)
            nc.vector.tensor_tensor(abs_tot[:, 2:3], abs_tot[:, 2:3], abs_tot[:, 3:4], ALU.add).then_inc(s_quant, 1)
            dve.wait_ge(s_quant, 2)
            nc.vector.tensor_scalar(gamma[:], abs_tot[:, 0:3], 1.0 / (FF * DIM), Q_EPS, ALU.mult, ALU.add
                                    ).then_inc(s_quant, 1)
            dve.wait_ge(s_quant, 3)
            nc.vector.tensor_scalar(half_gamma[:, 0, :], gamma[:], 0.5, None, ALU.mult)
            nc.vector.tensor_scalar(half_gamma[:, 1, :], gamma[:], -0.5, None, ALU.mult).then_inc(s_quant, 1)
            dve.wait_ge(s_quant, 4)
            dve.wait_ge(s_pads, 7)
            for i, (raw, q) in enumerate(((w1_raw[:], w1_q[:, :, 0:FF]), (w2_raw[:], w2_q[:, :, 0:FF]),
                                          (w3_raw[:, 0:FB - 1, :], w3_q[:, 0:FB - 1, :]),
                                          (w3_raw[0:FR, FB - 1:FB, :], w3_q[0:FR, FB - 1:FB, :]))):
                rows, n = raw.shape[0], raw.shape[1] * raw.shape[2]
                m = min(i, 2)
                is_below = below[0:rows, 0:n].rearrange("p (b c) -> p b c", b=raw.shape[1])
                if i:
                    dve.wait_ge(s_wq, i)
                nc.vector.tensor_scalar(is_below, raw, half_gamma[0:rows, 1, m:m + 1], None, ALU.is_lt
                                        ).then_inc(s_quant, 1)
                dve.wait_ge(s_quant, 5 + i)
                nc.vector.scalar_tensor_tensor(out=q, in0=raw, scalar=half_gamma[0:rows, 0, m:m + 1], in1=is_below,
                                               op0=ALU.is_gt, op1=ALU.subtract).then_inc(s_wq, 1)

            with dve.Fori(0, G) as g:
                for b in range(FB):
                    dve.wait_ge(s_sig, g * FB + b + 1)
                    if b >= 2:
                        dve.wait_ge(s_hidl, g * FB + b - 1)
                    nc.vector.tensor_tensor(hid[:, b % 2, :], ps_s[:, 2 * (b % 2) + 1, :], sig[:, b % 2, :],
                                            ALU.mult).then_inc(s_hid, 1)
                dve.wait_ge(s_down, g + 1)
                for j in range(TG):
                    tile = y[:, bass.ds(g * TG + j, 1), :].rearrange("p t c -> p (t c)")
                    nc.vector.tensor_tensor(tile, (ps_t if j < 2 else ps_o)[:, j % 2, 0:DIM], tile,
                                            ALU.add).then_inc(s_yacc, 1)

            def proj_low(n, lo, hi, half):
                col = slice(half * HALF, (half + 1) * HALF)
                dve.wait_ge(s_projh, n)
                nc.vector.tensor_tensor(lo[:, col], ps_s[:, 2 * half:2 * half + 2, :].rearrange("p b n -> p (b n)"),
                                        hi[:, col], ALU.subtract).then_inc(s_projl, 1)

            def value_low(h, bank, piece):
                kb = slice(piece * 4, piece * 4 + 4)
                dve.wait_ge(s_valh, VALS * h + piece + 1)
                nc.vector.tensor_tensor(v_lo[:, kb, :].rearrange("p k d -> p (k d)"), bank,
                                        v_hi[:, kb, :].rearrange("p k d -> p (k d)"), ALU.subtract).then_inc(s_vall, 1)

            def pt_low(h, t, half):
                kb = slice(half * KH, (half + 1) * KH)
                hi = (t % 2) * P
                lo = 2 * P + hi
                dve.wait_ge(s_pth, PT * h + 2 * t + half + 1)
                nc.vector.tensor_tensor(pt[:, (t // 2) % 2, kb, lo:lo + P],
                                        ps_t[:].rearrange("p b (k q) -> p (b k) q", q=P),
                                        pt[:, (t // 2) % 2, kb, hi:hi + P], ALU.subtract).then_inc(s_ptl, 1)

            def maximum(h, t):
                for half in (0, 1):
                    dve.wait_ge(s_scores, SCORES * h + 2 * t + half + 1)
                    nc.vector.reduce_max(row_max[:, t, half:half + 1],
                                         ps_s[:, 2 * half:2 * half + 2, :].rearrange("p b n -> p (b n)"),
                                         AX_X).then_inc(s_mx, 1)
                dve.wait_ge(s_mx, 2 * T * h + 2 * t + 2)
                nc.vector.tensor_scalar(neg_max[:, t:t + 1], row_max[:, t, 0:1], row_max[:, t, 1:2], -SCALE,
                                        ALU.max, ALU.mult).then_inc(s_nm, 1)

            def output_sum(h, p):
                dve.wait_ge(s_olow, PAIRS * h + p + 1)
                nc.vector.tensor_tensor(o_sum[:], ps_o[:, p % 2, 0:2 * P], o_low[:], ALU.add).then_inc(s_osum, 1)
                dve.wait_ge(s_exp, EXPS * h + 4 * p + 4)
                nc.vector.tensor_tensor(denom[:, 2 * p:2 * p + 2], row_sum[:, 2 * p:2 * p + 2, 0],
                                        row_sum[:, 2 * p:2 * p + 2, 1], ALU.add).then_inc(s_den, 1)

            def result(h, p):
                dve.wait_ge(s_den, PAIRS * h + p + 1)
                nc.vector.reciprocal(inv_denom[:, 2 * p:2 * p + 2], denom[:, 2 * p:2 * p + 2]).then_inc(s_inv, 1)
                dve.wait_ge(s_inv, PAIRS * h + p + 1)
                dve.wait_ge(s_y, PAIRS * h + p + 1)
                for j in range(2):
                    t = 2 * p + j
                    nc.vector.scalar_tensor_tensor(out=y[:, t, :], in0=ps_o[:, p % 2, j * DIM:(j + 1) * DIM],
                                                   scalar=inv_denom[:, t:t + 1], in1=y[:, t, :],
                                                   op0=ALU.mult, op1=ALU.add).then_inc(s_yacc, 1)

            for half in (0, 1):
                proj_low(half + 1, k_lo, k_hi, half)
            for half in (0, 1):
                proj_low(half + 3, q_lo, q_hi, half)

            def head(h, last_head):
                for t in range(T):
                    if t >= 2:
                        pt_low(h, t - 2, 1)
                    if t >= 5 and t % 2:
                        output_sum(h, (t - 5) // 2)
                    if t >= 6 and t % 2 == 0:
                        result(h, (t - 6) // 2)
                    maximum(h, t)
                    if t == 0:
                        value_low(h, ps_t[:, 0, :], 0)
                        value_low(h, ps_t[:, 1, :], 1)
                    if t == 2:
                        value_low(h, ps_o[:, 0, :], 2)
                    if t >= 1:
                        pt_low(h, t - 1, 0)
                    if t == 3:
                        value_low(h, ps_o[:, 1, :], 3)
                pt_low(h, T - 2, 1)
                result(h, 5)
                if not last_head:
                    for half in (0, 1):
                        proj_low(PROJ * (h + 1) + half + 1, k_lo, k_hi, half)
                pt_low(h, T - 1, 0)
                output_sum(h, 6)
                pt_low(h, T - 1, 1)
                if last_head:
                    result(h, 6)
                    output_sum(h, 7)
                else:
                    output_sum(h, 7)
                    proj_low(PROJ * (h + 1) + 3, q_lo, q_hi, 0)
                    result(h, 6)
                    proj_low(PROJ * (h + 1) + 4, q_lo, q_hi, 1)
                result(h, 7)

            with dve.Fori(0, H - 1) as h:
                head(h, False)
            head(H - 1, True)

        @block.gpsimd
        def _(pool):
            nc.gpsimd.memset(ident[:], 0.0).then_inc(s_pads, 1)
            nc.gpsimd.memset(abs_sum[:], 0.0).then_inc(s_pads, 1)
            nc.gpsimd.memset(w1_q[:, :, FF:FB * P].bitcast(F32), 0.0).then_inc(s_pads, 1)
            nc.gpsimd.memset(w2_q[:, :, FF:FB * P].bitcast(F32), 0.0).then_inc(s_pads, 1)
            pool.wait_ge(s_pads, 4)
            nc.gpsimd.memset(w3_q[FR:P, FB - 1, :].bitcast(F32), 0.0).then_inc(s_pads, 1)
            pool.wait_ge(s_pads, 5)
            nc.gpsimd.memset(ones[:], 1.0).then_inc(s_pads, 1)
            nc.gpsimd.memset(zeros[:], 0.0).then_inc(s_pads, 1)
            pool.wait_ge(s_pads, 7)
            nc.gpsimd.affine_select(out=ident[:], in_=ident[:], compare_op=ALU.not_equal, fill=1.0, base=0,
                                    pattern=[[-1, P]], channel_multiplier=1).then_inc(s_const, 1)

            def split_wqkv(n):
                pool.wait_ge(s_wqkv_in, 16 * n)
                nc.gpsimd.tensor_tensor(wqkv_hi[:], wqkv_raw[:], zeros[:], ALU.add).then_inc(s_whalf, 1)
                pool.wait_ge(s_whalf, n)
                nc.gpsimd.tensor_tensor(wqkv_lo[:], wqkv_raw[:], wqkv_hi[:], ALU.subtract).then_inc(s_wqkv, 1)

            def split_wo(n):
                pool.wait_ge(s_wo_in, 16 * n)
                nc.gpsimd.tensor_tensor(wo_hi[:], wo_raw[:], zeros[:, 0, 0:DIM], ALU.add).then_inc(s_wohalf, 1)
                pool.wait_ge(s_wohalf, n)
                nc.gpsimd.tensor_tensor(wo_lo[:], wo_raw[:], wo_hi[:], ALU.subtract).then_inc(s_wo, 1)

            with pool.Fori(0, G) as g:
                for b in range(FB):
                    pool.wait_ge(s_hidh, g * FB + b + 1)
                    nc.gpsimd.tensor_tensor(hid_lo[:, b, :], hid[:, b % 2, :], hid_hi[:, b, :],
                                            ALU.subtract).then_inc(s_hidl, 1)
            split_wqkv(1)
            split_wo(1)

            def head(h, last_head):
                for p in range(PAIRS):
                    if p == 1 and not last_head:
                        pool.wait_ge(s_val, VALS * h + 4)
                        split_wqkv(h + 2)
                    pool.wait_ge(s_osum, PAIRS * h + p + 1)
                    nc.gpsimd.tensor_tensor(o_hi[:], o_sum[:], zeros[:, 0, 0:2 * P], ALU.add).then_inc(s_ohi, 1)
                    pool.wait_ge(s_ohi, PAIRS * h + p + 1)
                    nc.gpsimd.tensor_tensor(o_lo[:], o_sum[:], o_hi[:], ALU.subtract).then_inc(s_osp, 1)
                if not last_head:
                    pool.wait_ge(s_y, PAIRS * h + 8)
                    split_wo(h + 2)

            with pool.Fori(0, H - 1) as h:
                head(h, False)
            head(H - 1, True)


def kernel(**inputs):
    import numpy as _np
    import concourse.bacc as _bacc
    from concourse.bass_utils import run_bass_kernel_spmd as _run

    nc = _bacc.Bacc("TRN2", target_bir_lowering=False, num_devices=1)
    wqkv = _np.asarray(inputs["L0_attn_Wqkv"]).reshape(3, H, D, C, P)
    arrays = {
        "x_dram": _np.asarray(inputs["L0_attn_x"]).reshape(S, DIM),
        "wqkv_dram": wqkv.transpose(1, 4, 3, 0, 2).reshape(H, P, C, 3 * D),
        "wo_dram": _np.asarray(inputs["L0_attn_Wout"]).T.reshape(H, P, DIM),
        "w1_dram": _np.asarray(inputs["L0_ffn_w1"]).T,
        "w2_dram": _np.asarray(inputs["L0_ffn_w2"]).T,
        "w3_dram": _np.asarray(inputs["L0_ffn_w3"]).T,
    }
    arrays = {k: _np.ascontiguousarray(v) for k, v in arrays.items()}
    args = [nc.dram_tensor(k, v.shape, F32, kind="ExternalInput").ap() for k, v in arrays.items()]
    args.append(nc.dram_tensor("out_dram", (S, DIM), F32, kind="ExternalOutput").ap())
    build(nc, *args)
    r = _run(nc, [arrays], core_ids=[0])
    return r.results[0]["out_dram"].reshape(1, S, DIM)
```

```python
import concourse.bass as bass
from concourse import mybir
from contextlib import ExitStack

F32 = mybir.dt.float32
F32R = mybir.dt.float32r
ALU = mybir.AluOpType
ACT = mybir.ActivationFunctionType
AX_X = mybir.AxisListType.X

P = 128
S = 2048
DIM = 256
H = 16
D = 128
FF = 704
C = DIM // P
T = S // P
PAIRS = T // 2
FB = -(-FF // P)
FR = FF - (FB - 1) * P
G = 4
CH = S // G
TG = CH // P
HALF = S // 2
KH = HALF // P
SCALE = float(D) ** -0.5
LN_EPS = 1e-5
Q_EPS = 1e-8

SCORES = EXPS = TRANS = PT = 2 * T
PROJ = 4
VALS = 4
YACC = T


def build(nc, x_d, wqkv_d, wo_d, w1_d, w2_d, w3_d, out_d):
    ctx = ExitStack()
    with ctx:
        def sb(name, shape, dt=F32, where=ctx):
            return where.enter_context(nc.sbuf_tensor(name, shape, dt))

        def sem(name):
            return ctx.enter_context(nc.semaphore(name))

        y = sb("y", [P, T, DIM])
        xt_hi = sb("xt_hi", [P, C, S], F32R)
        xt_lo = sb("xt_lo", [P, C, S], F32R)
        k_hi = sb("k_hi", [P, S], F32R)
        k_lo = sb("k_lo", [P, S], F32R)
        q_hi = sb("q_hi", [P, S], F32R)
        q_lo = sb("q_lo", [P, S], F32R)
        v_hi = sb("v_hi", [P, T, D], F32R)
        v_lo = sb("v_lo", [P, T, D], F32R)
        wqkv_raw = sb("wqkv_raw", [P, C, 3 * D])
        wqkv = sb("wqkv", [P, C, 2, 3 * D], F32R)
        wo_raw = sb("wo_raw", [P, DIM])
        wo_hi = sb("wo_hi", [P, DIM], F32R)
        wo_lo = sb("wo_lo", [P, DIM], F32R)
        v_low = sb("v_low", [P, 4 * D])
        v_sum = sb("v_sum", [P, 2, 4 * D])
        o_low = sb("o_low", [P, 2 * P])
        o_sum = sb("o_sum", [P, 2 * P])
        o_hi = sb("o_hi", [P, 2 * P], F32R)
        o_lo = sb("o_lo", [P, 2 * P], F32R)
        ident = sb("ident", [P, P])
        zeros = sb("zeros", [P, C, 3 * D])
        zeros_v = zeros[:].rearrange("p c e -> p (c e)")[:, 0:4 * D].rearrange("p (k d) -> p k d", d=D)
        row_max = sb("row_max", [P, T, 2])
        neg_max = sb("neg_max", [P, T])
        row_sum = sb("row_sum", [P, T, 2])
        denom = sb("denom", [P, T])
        inv_denom = sb("inv_denom", [P, T])

        with ExitStack() as early:
            w1_raw = sb("w1_raw", [P, C, FF], where=early)
            w2_raw = sb("w2_raw", [P, C, FF], where=early)
            w3_raw = sb("w3_raw", [P, FB, DIM], where=early)
            w1_q = sb("w1_q", [P, C, FB * P], F32R, early)
            w2_q = sb("w2_q", [P, C, FB * P], F32R, early)
            w3_q = sb("w3_q", [P, FB, DIM], F32R, early)
            ones = sb("ones", [P, P], where=early)
            abs_sum = sb("abs_sum", [P, 4], where=early)
            abs_tot = sb("abs_tot", [P, 4], where=early)
            gamma = sb("gamma", [P, 3], where=early)
            half_gamma = sb("half_gamma", [P, 2, 3], where=early)
            stats = sb("stats", [P, T, 6], where=early)
            mean = sb("mean", [P, T], where=early)
            diff = sb("diff", [P, T], where=early)
            var_eps = sb("var_eps", [P, T], where=early)
            std = sb("std", [P, T], where=early)
            rstd = sb("rstd", [P, T], where=early)
            newton = sb("newton", [P, T], where=early)
            sig = sb("sig", [P, 2, CH], where=early)
            hid = sb("hid", [P, 2, CH], where=early)
            with ExitStack() as first:
                xn = sb("xn", [P, T, DIM], where=first)
                below = sb("below", [P, FB * DIM], where=first)
            hid_hi = sb("hid_hi", [P, FB, CH], F32R, early)
            hid_lo = sb("hid_lo", [P, FB, CH], F32R, early)
            junk = hid_lo[:].rearrange("p b n -> p (b n)")
        prob = sb("prob", [P, 2, S])
        pt = sb("pt", [P, 2, T, 4 * P], F32R)

        ps_s = ctx.enter_context(nc.psum_tensor("ps_s", [P, 4, 512], F32))
        ps_t = ctx.enter_context(nc.psum_tensor("ps_t", [P, 2, 512], F32))
        ps_o = ctx.enter_context(nc.psum_tensor("ps_o", [P, 2, 512], F32))

        s_x = [sem(f"x{g}_loaded") for g in range(G)]
        s_w = [sem("w1_loaded"), sem("w2_loaded"), sem("w3_loaded")]
        s_wqkv_in = sem("wqkv_loaded")
        s_wo_in = sem("wo_loaded")
        s_const = sem("constants_ready")
        s_pads = sem("pads_zeroed")
        s_abs = sem("abs_sums_ready")
        s_tot = sem("abs_totals_ready")
        s_quant = sem("rounded_signs_ready")
        s_wq = sem("quantised_weights_ready")
        s_ln = sem("layernorm_step_done")
        s_std = sem("std_ready")
        s_xn = sem("normalised_ready")
        s_xtr = sem("normalised_transposed")
        s_xth = sem("xt_high_ready")
        s_xtl = sem("xt_low_ready")
        s_up = sem("ffn_up_done")
        s_sig = sem("sigmoid_ready")
        s_hid = sem("hidden_ready")
        s_hidh = sem("hidden_high_ready")
        s_hidl = sem("hidden_low_ready")
        s_down = sem("ffn_down_done")
        s_wqkv = sem("wqkv_split")
        s_whalf = sem("wqkv_high_ready")
        s_wo = sem("wo_split")
        s_wohalf = sem("wo_high_ready")
        s_proj = sem("keys_queries_done")
        s_projh = sem("keys_queries_high_ready")
        s_projl = sem("keys_queries_low_ready")
        s_val = sem("values_done")
        s_vlow = sem("low_values_copied")
        s_vsum = sem("values_summed")
        s_vhi = sem("values_high_ready")
        s_vsplit = sem("values_split")
        s_scores = sem("logits_done")
        s_mx = sem("half_max_ready")
        s_nm = sem("neg_max_ready")
        s_exp = sem("exponentials_ready")
        s_tr = sem("transposes_done")
        s_pth = sem("pt_high_ready")
        s_ptl = sem("pt_low_ready")
        s_pv = sem("values_product_done")
        s_olow = sem("low_output_copied")
        s_osum = sem("output_summed")
        s_ohi = sem("output_high_ready")
        s_osp = sem("output_split")
        s_den = sem("denominator_ready")
        s_inv = sem("inverse_ready")
        s_y = sem("projection_done")
        s_yacc = sem("result_added")
        s_out = sem("result_stored")

        block = ctx.enter_context(nc.Block())

        @block.sync
        def _(sp):
            x_v = x_d.rearrange("(t p) c -> p t c", p=P)
            for g in range(G):
                sp.dma_start(y[:, g * TG:(g + 1) * TG, :], x_v[:, g * TG:(g + 1) * TG, :]).then_inc(s_x[g], 16)
                if g == 0:
                    sp.dma_start(w1_raw[:], w1_d.rearrange("(c p) f -> p c f", p=P)).then_inc(s_w[0], 16)
                    sp.dma_start(w2_raw[:], w2_d.rearrange("(c p) f -> p c f", p=P)).then_inc(s_w[1], 16)
            sp.dma_start(w3_raw[:, 0:FB - 1, :],
                         w3_d[0:(FB - 1) * P, :].rearrange("(b p) c -> p b c", p=P)).then_inc(s_w[2], 16)
            sp.dma_start(w3_raw[0:FR, FB - 1, :], w3_d[(FB - 1) * P:FF, :]).then_inc(s_w[2], 16)
            sp.dma_start(wqkv_raw[:], wqkv_d[0:1].rearrange("h p c e -> p (h c) e")).then_inc(s_wqkv_in, 16)
            sp.dma_start(wo_raw[:], wo_d[0:1].rearrange("h p c -> p (h c)")).then_inc(s_wo_in, 16)
            with sp.Fori(0, H - 1) as h:
                sp.wait_ge(s_wqkv, h + 1)
                sp.dma_start(wqkv_raw[:],
                             wqkv_d[bass.ds(h + 1, 1)].rearrange("h p c e -> p (h c) e")).then_inc(s_wqkv_in, 16)
                sp.wait_ge(s_wo, h + 1)
                sp.dma_start(wo_raw[:],
                             wo_d[bass.ds(h + 1, 1)].rearrange("h p c -> p (h c)")).then_inc(s_wo_in, 16)
            out_v = out_d.rearrange("(t p) c -> p t c", p=P)
            for p in range(PAIRS):
                sp.wait_ge(s_yacc, YACC * H + 2 * p + 2)
                sp.dma_start(out_v[:, 2 * p:2 * p + 2, :], y[:, 2 * p:2 * p + 2, :]).then_inc(s_out, 16)
            sp.wait_ge(s_out, 16 * PAIRS)

        @block.tensor
        def _(pe):
            def project(first, part, half):
                for bank in (2 * half, 2 * half + 1):
                    col = slice(bank * 512, bank * 512 + 512)
                    n = 0
                    for c in range(C):
                        for w, x in ((0, xt_hi), (0, xt_lo), (1, xt_hi)):
                            last = nc.tensor.matmul(ps_s[:, bank, :], wqkv[:, c, w, part * D:(part + 1) * D],
                                                    x[:, c, col], start=(n == 0), stop=(n == 3 * C - 1))
                            n += 1
                last.then_inc(s_proj, 1)

            def values(banks, piece):
                for j in range(4):
                    kb = piece * 4 + j
                    dst = banks[:, j // 2, (j % 2) * 2 * D:(j % 2 + 1) * 2 * D]
                    for c in range(C):
                        nc.tensor.matmul(dst.rearrange("p (a d) -> p a d", d=D), xt_hi[:, c, kb * P:(kb + 1) * P],
                                         wqkv[:, c, :, 2 * D:3 * D], start=(c == 0), stop=(c == C - 1),
                                         skip_group_check=True)
                        last = nc.tensor.matmul(dst[:, 0:D], xt_lo[:, c, kb * P:(kb + 1) * P],
                                                wqkv[:, c, 0, 2 * D:3 * D], start=False, stop=(c == C - 1),
                                                skip_group_check=True)
                last.then_inc(s_val, 1)

            def logits(t, half):
                for bank in (2 * half, 2 * half + 1):
                    col = slice(bank * 512, bank * 512 + 512)
                    tile = slice(t * P, (t + 1) * P)
                    nc.tensor.matmul(ps_s[:, bank, :], q_hi[:, tile], k_hi[:, col], start=True, stop=False)
                    nc.tensor.matmul(ps_s[:, bank, :], q_hi[:, tile], k_lo[:, col], start=False, stop=False)
                    last = nc.tensor.matmul(ps_s[:, bank, :], q_lo[:, tile], k_hi[:, col], start=False, stop=True)
                last.then_inc(s_scores, 1)

            def transposes(t, half):
                for i in range(KH):
                    kb = half * KH + i
                    last = nc.tensor.transpose(ps_t[:, i // 4, (i % 4) * P:(i % 4 + 1) * P],
                                               prob[:, t % 2, kb * P:(kb + 1) * P], ident[:])
                last.then_inc(s_tr, 1)

            def products(p, half):
                for i in range(KH):
                    kb = half * KH + i
                    nc.tensor.matmul(ps_o[:, p % 2, :], v_hi[:, kb, :], pt[:, p % 2, kb, :],
                                     start=(kb == 0), stop=(kb == T - 1), skip_group_check=True)
                    last = nc.tensor.matmul(ps_o[:, p % 2, 0:2 * P], v_lo[:, kb, :], pt[:, p % 2, kb, 0:2 * P],
                                            start=False, stop=(kb == T - 1), skip_group_check=True)
                if half:
                    last.then_inc(s_pv, 1)

            def out_projection(p):
                for j in range(2):
                    tile = slice(j * P, (j + 1) * P)
                    dst = ps_o[:, p % 2, j * DIM:(j + 1) * DIM]
                    nc.tensor.matmul(dst, o_hi[:, tile], wo_hi[:], start=True, stop=False)
                    nc.tensor.matmul(dst, o_hi[:, tile], wo_lo[:], start=False, stop=False)
                    last = nc.tensor.matmul(dst, o_lo[:, tile], wo_hi[:], start=False, stop=True)
                last.then_inc(s_y, 1)

            pe.wait_ge(s_const, 1)
            pe.wait_ge(s_abs, 4)
            nc.tensor.matmul(ps_o[:, 0, 0:4], ones[:], abs_sum[:], start=True, stop=True).then_inc(s_tot, 1)
            pe.wait_ge(s_const, 1)
            for g in range(G):
                pe.wait_ge(s_xn, g + 1)
                for c in range(C):
                    if g:
                        pe.wait_ge(s_xtl, C * (g - 1) + c + 1)
                    for j in range(TG):
                        last = nc.tensor.transpose(ps_t[:, c, j * P:(j + 1) * P],
                                                   xn[:, g * TG + j, c * P:(c + 1) * P], ident[:])
                    last.then_inc(s_xtr, 1)

            def ffn_up(g):
                for b in range(FB):
                    if b >= 2:
                        pe.wait_ge(s_hid, g * FB + b - 1)
                    for w, k in ((w1_q, 0), (w2_q, 1)):
                        n = 0
                        for c in range(C):
                            for x in (xt_hi, xt_lo):
                                last = nc.tensor.matmul(ps_s[:, 2 * (b % 2) + k, :], w[:, c, b * P:(b + 1) * P],
                                                        x[:, c, bass.ds(g * CH, CH)],
                                                        start=(n == 0), stop=(n == 2 * C - 1))
                                n += 1
                    last.then_inc(s_up, 1)

            def ffn_down(g):
                for b in range(FB):
                    pe.wait_ge(s_hidl, g * FB + b + 1)
                    for j in range(TG):
                        dst = (ps_t if j < 2 else ps_o)[:, j % 2, 0:DIM]
                        nc.tensor.matmul(dst, hid_hi[:, b, j * P:(j + 1) * P], w3_q[:, b, :],
                                         start=(b == 0), stop=False)
                        last = nc.tensor.matmul(dst, hid_lo[:, b, j * P:(j + 1) * P], w3_q[:, b, :],
                                                start=False, stop=(b == FB - 1))
                last.then_inc(s_down, 1)

            pe.wait_ge(s_wq, 2)
            pe.wait_ge(s_xtl, C)
            ffn_up(0)
            pe.wait_ge(s_wq, 4)
            pe.wait_ge(s_xtl, C * G)
            ffn_down(0)
            with pe.Fori(1, G) as g:
                ffn_up(g)
                pe.wait_ge(s_yacc, TG * g)
                ffn_down(g)
            pe.wait_ge(s_yacc, YACC)
            pe.wait_ge(s_wqkv, 1)
            for part in (1, 0):
                for half in (0, 1):
                    if part == 0:
                        pe.wait_ge(s_projl, half + 1)
                    project(0, part, half)

            def head(h, last_head):
                for t in range(T):
                    for half in (0, 1):
                        if t == 0:
                            pe.wait_ge(s_projl, PROJ * h + 3 + half)
                        else:
                            pe.wait_ge(s_exp, EXPS * h + 2 * (t - 1) + half + 1)
                        logits(t, half)
                    if t == 0:
                        pe.wait_ge(s_wqkv, h + 1)
                        values(ps_t, 0)
                        pe.wait_ge(s_yacc, YACC * h + 16)
                        values(ps_o, 1)
                    if t >= 1:
                        if t == 1:
                            pe.wait_ge(s_vsum, VALS * h + 1)
                        else:
                            pe.wait_ge(s_ptl, PT * h + 2 * (t - 1))
                        pe.wait_ge(s_exp, EXPS * h + 2 * (t - 1) + 1)
                        transposes(t - 1, 0)
                    if t == 1:
                        pe.wait_ge(s_vsum, VALS * h + 2)
                        values(ps_o, 2)
                    if t == 2:
                        pe.wait_ge(s_vsum, VALS * h + 3)
                        values(ps_o, 3)
                    if t >= 3 and t % 2:
                        p = (t - 3) // 2
                        if p == 0:
                            pe.wait_ge(s_vsum, VALS * h + 4)
                            pe.wait_ge(s_vsplit, VALS * h + 2)
                        if p >= 2:
                            pe.wait_ge(s_yacc, YACC * h + 16 + 2 * (p - 1))
                        pe.wait_ge(s_ptl, PT * h + 4 * p + 3)
                        products(p, 0)
                    if t >= 4 and t % 2 == 0:
                        p = (t - 4) // 2
                        if p == 0:
                            pe.wait_ge(s_vsplit, VALS * h + 4)
                        pe.wait_ge(s_ptl, PT * h + 4 * p + 4)
                        products(p, 1)
                    if t >= 5 and t % 2:
                        p = (t - 5) // 2
                        if p == 0:
                            pe.wait_ge(s_wo, h + 1)
                        pe.wait_ge(s_osp, PAIRS * h + p + 1)
                        out_projection(p)
                    if t >= 1:
                        pe.wait_ge(s_ptl, PT * h + 2 * (t - 1) + 1)
                        pe.wait_ge(s_exp, EXPS * h + 2 * (t - 1) + 2)
                        transposes(t - 1, 1)
                if not last_head:
                    pe.wait_ge(s_wqkv, h + 2)
                    for half in (0, 1):
                        pe.wait_ge(s_exp, EXPS * h + 2 * (T - 1) + half + 1)
                        project(h, 1, half)
                pe.wait_ge(s_ptl, PT * h + 2 * (T - 1))
                pe.wait_ge(s_exp, EXPS * h + 2 * (T - 1) + 1)
                transposes(T - 1, 0)
                pe.wait_ge(s_ptl, PT * h + 4 * 6 + 4)
                products(6, 1)
                pe.wait_ge(s_ptl, PT * h + 2 * (T - 1) + 1)
                pe.wait_ge(s_exp, EXPS * h + 2 * (T - 1) + 2)
                transposes(T - 1, 1)
                pe.wait_ge(s_yacc, YACC * h + 16 + 2 * 6)
                products(7, 0)
                pe.wait_ge(s_osp, PAIRS * h + 7)
                out_projection(6)
                pe.wait_ge(s_ptl, PT * h + 2 * T)
                products(7, 1)
                if not last_head:
                    for half in (0, 1):
                        pe.wait_ge(s_projl, PROJ * (h + 1) + half + 1)
                        project(h, 0, half)
                pe.wait_ge(s_osp, PAIRS * h + 8)
                out_projection(7)

            with pe.Fori(0, H - 1) as h:
                head(h, False)
            head(H - 1, True)

        @block.scalar
        def _(act):
            act.wait_ge(s_const, 1)
            for i, w in enumerate((w1_raw, w2_raw)):
                act.wait_ge(s_w[i], 16)
                if i:
                    act.wait_ge(s_abs, i)
                nc.scalar.activation(junk[:, 0:C * FF], w[:].rearrange("p c f -> p (c f)"), ACT.Abs,
                                     accum_out=abs_sum[:, i:i + 1]).then_inc(s_abs, 1)
            act.wait_ge(s_w[2], 32)
            act.wait_ge(s_abs, 2)
            nc.scalar.activation(junk[:, 0:(FB - 1) * DIM], w3_raw[:, 0:FB - 1, :].rearrange("p b c -> p (b c)"), ACT.Abs,
                                 accum_out=abs_sum[:, 2:3]).then_inc(s_abs, 1)
            act.wait_ge(s_abs, 3)
            nc.scalar.activation(junk[0:FR, 0:DIM], w3_raw[0:FR, FB - 1, :], ACT.Abs,
                                 accum_out=abs_sum[0:FR, 3:4]).then_inc(s_abs, 1)
            act.wait_ge(s_ln, 4)
            nc.scalar.activation(std[:], var_eps[:], ACT.Sqrt).then_inc(s_std, 1)
            with act.Fori(0, G) as g:
                for c in range(C):
                    act.wait_ge(s_xtr, C * g + c + 1)
                    nc.scalar.copy(xt_hi[:, c, bass.ds(g * CH, CH)], ps_t[:, c, :]).then_inc(s_xth, 1)
            with act.Fori(0, G) as g:
                for b in range(FB + 1):
                    if b < FB:
                        act.wait_ge(s_up, g * FB + b + 1)
                        if b >= 2:
                            act.wait_ge(s_hid, g * FB + b - 1)
                        nc.scalar.activation(sig[:, b % 2, :], ps_s[:, 2 * (b % 2), :], ACT.Sigmoid
                                             ).then_inc(s_sig, 1)
                    if b >= 1:
                        act.wait_ge(s_hid, g * FB + b)
                        nc.scalar.copy(hid_hi[:, b - 1, :], hid[:, (b - 1) % 2, :]).then_inc(s_hidh, 1)

            def proj_high(n, dst, half):
                act.wait_ge(s_proj, n)
                nc.scalar.copy(dst[:, half * HALF:(half + 1) * HALF],
                               ps_s[:, 2 * half:2 * half + 2, :].rearrange("p b n -> p (b n)")).then_inc(s_projh, 1)

            def low_values(h, banks, piece):
                act.wait_ge(s_val, VALS * h + piece + 1)
                if piece:
                    act.wait_ge(s_vsum, VALS * h + piece)
                nc.scalar.copy(v_low[:].rearrange("p (k d) -> p k d", d=D),
                               banks[:].rearrange("p b (k n) -> p (b k) n", n=2 * D)[:, :, D:2 * D]
                               ).then_inc(s_vlow, 1)

            def pt_high(h, t, half):
                act.wait_ge(s_tr, TRANS * h + 2 * t + half + 1)
                nc.scalar.copy(pt[:, (t // 2) % 2, half * KH:(half + 1) * KH, (t % 2) * P:(t % 2 + 1) * P],
                               ps_t[:].rearrange("p b (k q) -> p (b k) q", q=P)).then_inc(s_pth, 1)

            def exponential(h, t, half):
                act.wait_ge(s_nm, T * h + t + 1)
                nc.scalar.activation(prob[:, t % 2, half * HALF:(half + 1) * HALF],
                                     ps_s[:, 2 * half:2 * half + 2, :].rearrange("p b n -> p (b n)"), ACT.Exp,
                                     bias=neg_max[:, t:t + 1], scale=SCALE,
                                     accum_out=row_sum[:, t, half:half + 1]).then_inc(s_exp, 1)

            def low_output(h, p):
                act.wait_ge(s_pv, PAIRS * h + p + 1)
                nc.scalar.copy(o_low[:], ps_o[:, p % 2, 2 * P:4 * P]).then_inc(s_olow, 1)

            for half in (0, 1):
                proj_high(half + 1, k_hi, half)
            for half in (0, 1):
                proj_high(half + 3, q_hi, half)

            def head(h, last_head):
                for t in range(T):
                    if t >= 2:
                        pt_high(h, t - 2, 1)
                    if t >= 5 and t % 2:
                        low_output(h, (t - 5) // 2)
                    if t >= 1:
                        pt_high(h, t - 1, 0)
                    exponential(h, t, 0)
                    exponential(h, t, 1)
                    if t == 0:
                        low_values(h, ps_t, 0)
                        low_values(h, ps_o, 1)
                    if t in (1, 2):
                        low_values(h, ps_o, t + 1)
                pt_high(h, T - 2, 1)
                if not last_head:
                    for half in (0, 1):
                        proj_high(PROJ * (h + 1) + half + 1, k_hi, half)
                pt_high(h, T - 1, 0)
                low_output(h, 6)
                pt_high(h, T - 1, 1)
                low_output(h, 7)
                if not last_head:
                    for half in (0, 1):
                        proj_high(PROJ * (h + 1) + half + 3, q_hi, half)

            with act.Fori(0, H - 1) as h:
                head(h, False)
            head(H - 1, True)

        @block.vector
        def _(dve):
            for t in range(T):
                if t % TG == 0:
                    dve.wait_ge(s_x[t // TG], 16)
                last = nc.vector.bn_stats(stats[:, t, :], y[:, t, :])
            last.then_inc(s_ln, 1)
            dve.wait_ge(s_ln, 1)
            nc.vector.tensor_tensor(mean[:], stats[:, :, 1], stats[:, :, 4], ALU.add)
            nc.vector.tensor_tensor(diff[:], stats[:, :, 1], stats[:, :, 4], ALU.subtract)
            nc.vector.tensor_tensor(var_eps[:], stats[:, :, 2], stats[:, :, 5], ALU.add).then_inc(s_ln, 1)
            dve.wait_ge(s_ln, 2)
            nc.vector.tensor_scalar(mean[:], mean[:], 0.5, None, ALU.mult)
            nc.vector.tensor_tensor(diff[:], diff[:], diff[:], ALU.mult)
            nc.vector.tensor_scalar(var_eps[:], var_eps[:], 1.0 / DIM, LN_EPS, ALU.mult, ALU.add).then_inc(s_ln, 1)
            dve.wait_ge(s_ln, 3)
            nc.vector.scalar_tensor_tensor(out=var_eps[:], in0=diff[:], scalar=0.25, in1=var_eps[:],
                                           op0=ALU.mult, op1=ALU.add).then_inc(s_ln, 1)
            dve.wait_ge(s_std, 1)
            nc.vector.reciprocal(rstd[:], std[:]).then_inc(s_ln, 1)
            dve.wait_ge(s_ln, 5)
            nc.vector.tensor_tensor(newton[:], rstd[:], rstd[:], ALU.mult).then_inc(s_ln, 1)
            dve.wait_ge(s_ln, 6)
            nc.vector.tensor_tensor(newton[:], newton[:], var_eps[:], ALU.mult).then_inc(s_ln, 1)
            dve.wait_ge(s_ln, 7)
            nc.vector.tensor_scalar(newton[:], newton[:], -0.5, 1.5, ALU.mult, ALU.add).then_inc(s_ln, 1)
            dve.wait_ge(s_ln, 8)
            nc.vector.tensor_tensor(rstd[:], rstd[:], newton[:], ALU.mult).then_inc(s_ln, 1)
            dve.wait_ge(s_ln, 9)
            for t in range(T):
                last = nc.vector.tensor_scalar(xn[:, t, :], y[:, t, :], mean[:, t:t + 1], rstd[:, t:t + 1],
                                               ALU.subtract, ALU.mult)
                if t % TG == TG - 1:
                    last.then_inc(s_xn, 1)
            with dve.Fori(0, G) as g:
                for c in range(C):
                    dve.wait_ge(s_xth, C * g + c + 1)
                    nc.vector.tensor_tensor(xt_lo[:, c, bass.ds(g * CH, CH)], ps_t[:, c, :],
                                            xt_hi[:, c, bass.ds(g * CH, CH)], ALU.subtract).then_inc(s_xtl, 1)

            dve.wait_ge(s_tot, 1)
            nc.vector.tensor_copy(abs_tot[:], ps_o[:, 0, 0:4]).then_inc(s_quant, 1)
            dve.wait_ge(s_quant, 1)
            nc.vector.tensor_tensor(abs_tot[:, 2:3], abs_tot[:, 2:3], abs_tot[:, 3:4], ALU.add).then_inc(s_quant, 1)
            dve.wait_ge(s_quant, 2)
            nc.vector.tensor_scalar(gamma[:], abs_tot[:, 0:3], 1.0 / (FF * DIM), Q_EPS, ALU.mult, ALU.add
                                    ).then_inc(s_quant, 1)
            dve.wait_ge(s_quant, 3)
            nc.vector.tensor_scalar(half_gamma[:, 0, :], gamma[:], 0.5, None, ALU.mult)
            nc.vector.tensor_scalar(half_gamma[:, 1, :], gamma[:], -0.5, None, ALU.mult).then_inc(s_quant, 1)
            dve.wait_ge(s_quant, 4)
            dve.wait_ge(s_pads, 7)
            for i, (raw, q) in enumerate(((w1_raw[:], w1_q[:, :, 0:FF]), (w2_raw[:], w2_q[:, :, 0:FF]),
                                          (w3_raw[:, 0:FB - 1, :], w3_q[:, 0:FB - 1, :]),
                                          (w3_raw[0:FR, FB - 1:FB, :], w3_q[0:FR, FB - 1:FB, :]))):
                rows, n = raw.shape[0], raw.shape[1] * raw.shape[2]
                m = min(i, 2)
                is_below = below[0:rows, 0:n].rearrange("p (b c) -> p b c", b=raw.shape[1])
                if i:
                    dve.wait_ge(s_wq, i)
                nc.vector.tensor_scalar(is_below, raw, half_gamma[0:rows, 1, m:m + 1], None, ALU.is_lt
                                        ).then_inc(s_quant, 1)
                dve.wait_ge(s_quant, 5 + i)
                nc.vector.scalar_tensor_tensor(out=q, in0=raw, scalar=half_gamma[0:rows, 0, m:m + 1], in1=is_below,
                                               op0=ALU.is_gt, op1=ALU.subtract).then_inc(s_wq, 1)

            with dve.Fori(0, G) as g:
                for b in range(FB):
                    dve.wait_ge(s_sig, g * FB + b + 1)
                    if b >= 2:
                        dve.wait_ge(s_hidl, g * FB + b - 1)
                    nc.vector.tensor_tensor(hid[:, b % 2, :], ps_s[:, 2 * (b % 2) + 1, :], sig[:, b % 2, :],
                                            ALU.mult).then_inc(s_hid, 1)
                dve.wait_ge(s_down, g + 1)
                for j in range(TG):
                    tile = y[:, bass.ds(g * TG + j, 1), :].rearrange("p t c -> p (t c)")
                    nc.vector.tensor_tensor(tile, (ps_t if j < 2 else ps_o)[:, j % 2, 0:DIM], tile,
                                            ALU.add).then_inc(s_yacc, 1)

            def proj_low(n, lo, hi, half):
                col = slice(half * HALF, (half + 1) * HALF)
                dve.wait_ge(s_projh, n)
                nc.vector.tensor_tensor(lo[:, col], ps_s[:, 2 * half:2 * half + 2, :].rearrange("p b n -> p (b n)"),
                                        hi[:, col], ALU.subtract).then_inc(s_projl, 1)

            def values_sum(h, banks, piece):
                dve.wait_ge(s_vlow, VALS * h + piece + 1)
                if piece >= 2:
                    dve.wait_ge(s_vsplit, VALS * h + piece - 1)
                nc.vector.tensor_tensor(v_sum[:, piece % 2, :].rearrange("p (k d) -> p k d", d=D),
                                        banks[:].rearrange("p b (k n) -> p (b k) n", n=2 * D)[:, :, 0:D],
                                        v_low[:].rearrange("p (k d) -> p k d", d=D), ALU.add).then_inc(s_vsum, 1)

            def pt_low(h, t, half):
                kb = slice(half * KH, (half + 1) * KH)
                hi = (t % 2) * P
                lo = 2 * P + hi
                dve.wait_ge(s_pth, PT * h + 2 * t + half + 1)
                nc.vector.tensor_tensor(pt[:, (t // 2) % 2, kb, lo:lo + P],
                                        ps_t[:].rearrange("p b (k q) -> p (b k) q", q=P),
                                        pt[:, (t // 2) % 2, kb, hi:hi + P], ALU.subtract).then_inc(s_ptl, 1)

            def maximum(h, t):
                for half in (0, 1):
                    dve.wait_ge(s_scores, SCORES * h + 2 * t + half + 1)
                    nc.vector.reduce_max(row_max[:, t, half:half + 1],
                                         ps_s[:, 2 * half:2 * half + 2, :].rearrange("p b n -> p (b n)"),
                                         AX_X).then_inc(s_mx, 1)
                dve.wait_ge(s_mx, 2 * T * h + 2 * t + 2)
                nc.vector.tensor_scalar(neg_max[:, t:t + 1], row_max[:, t, 0:1], row_max[:, t, 1:2], -SCALE,
                                        ALU.max, ALU.mult).then_inc(s_nm, 1)

            def output_sum(h, p):
                dve.wait_ge(s_olow, PAIRS * h + p + 1)
                nc.vector.tensor_tensor(o_sum[:], ps_o[:, p % 2, 0:2 * P], o_low[:], ALU.add).then_inc(s_osum, 1)
                dve.wait_ge(s_exp, EXPS * h + 4 * p + 4)
                nc.vector.tensor_tensor(denom[:, 2 * p:2 * p + 2], row_sum[:, 2 * p:2 * p + 2, 0],
                                        row_sum[:, 2 * p:2 * p + 2, 1], ALU.add).then_inc(s_den, 1)

            def result(h, p):
                dve.wait_ge(s_den, PAIRS * h + p + 1)
                nc.vector.reciprocal(inv_denom[:, 2 * p:2 * p + 2], denom[:, 2 * p:2 * p + 2]).then_inc(s_inv, 1)
                dve.wait_ge(s_inv, PAIRS * h + p + 1)
                dve.wait_ge(s_y, PAIRS * h + p + 1)
                for j in range(2):
                    t = 2 * p + j
                    nc.vector.scalar_tensor_tensor(out=y[:, t, :], in0=ps_o[:, p % 2, j * DIM:(j + 1) * DIM],
                                                   scalar=inv_denom[:, t:t + 1], in1=y[:, t, :],
                                                   op0=ALU.mult, op1=ALU.add).then_inc(s_yacc, 1)

            for half in (0, 1):
                proj_low(half + 1, k_lo, k_hi, half)
            for half in (0, 1):
                proj_low(half + 3, q_lo, q_hi, half)

            def head(h, last_head):
                for t in range(T):
                    if t >= 2:
                        pt_low(h, t - 2, 1)
                    if t >= 5 and t % 2:
                        output_sum(h, (t - 5) // 2)
                    maximum(h, t)
                    if t == 0:
                        values_sum(h, ps_t, 0)
                        values_sum(h, ps_o, 1)
                    if t >= 1:
                        pt_low(h, t - 1, 0)
                    if t in (1, 2):
                        values_sum(h, ps_o, t + 1)
                    if t >= 6 and t % 2 == 0:
                        result(h, (t - 6) // 2)
                pt_low(h, T - 2, 1)
                result(h, 5)
                if not last_head:
                    for half in (0, 1):
                        proj_low(PROJ * (h + 1) + half + 1, k_lo, k_hi, half)
                pt_low(h, T - 1, 0)
                output_sum(h, 6)
                pt_low(h, T - 1, 1)
                if last_head:
                    result(h, 6)
                    output_sum(h, 7)
                else:
                    output_sum(h, 7)
                    proj_low(PROJ * (h + 1) + 3, q_lo, q_hi, 0)
                    result(h, 6)
                    proj_low(PROJ * (h + 1) + 4, q_lo, q_hi, 1)
                result(h, 7)

            with dve.Fori(0, H - 1) as h:
                head(h, False)
            head(H - 1, True)

        @block.gpsimd
        def _(pool):
            nc.gpsimd.memset(ident[:], 0.0).then_inc(s_pads, 1)
            nc.gpsimd.memset(abs_sum[:], 0.0).then_inc(s_pads, 1)
            nc.gpsimd.memset(w1_q[:, :, FF:FB * P].bitcast(F32), 0.0).then_inc(s_pads, 1)
            nc.gpsimd.memset(w2_q[:, :, FF:FB * P].bitcast(F32), 0.0).then_inc(s_pads, 1)
            pool.wait_ge(s_pads, 4)
            nc.gpsimd.memset(w3_q[FR:P, FB - 1, :].bitcast(F32), 0.0).then_inc(s_pads, 1)
            pool.wait_ge(s_pads, 5)
            nc.gpsimd.memset(ones[:], 1.0).then_inc(s_pads, 1)
            nc.gpsimd.memset(zeros[:], 0.0).then_inc(s_pads, 1)
            pool.wait_ge(s_pads, 7)
            nc.gpsimd.affine_select(out=ident[:], in_=ident[:], compare_op=ALU.not_equal, fill=1.0, base=0,
                                    pattern=[[-1, P]], channel_multiplier=1).then_inc(s_const, 1)

            def split_wqkv(n):
                pool.wait_ge(s_wqkv_in, 16 * n)
                nc.gpsimd.tensor_tensor(wqkv[:, :, 0, :], wqkv_raw[:], zeros[:], ALU.add).then_inc(s_whalf, 1)
                pool.wait_ge(s_whalf, n)
                nc.gpsimd.tensor_tensor(wqkv[:, :, 1, :], wqkv_raw[:], wqkv[:, :, 0, :], ALU.subtract
                                        ).then_inc(s_wqkv, 1)

            def split_wo(n):
                pool.wait_ge(s_wo_in, 16 * n)
                nc.gpsimd.tensor_tensor(wo_hi[:], wo_raw[:], zeros[:, 0, 0:DIM], ALU.add).then_inc(s_wohalf, 1)
                pool.wait_ge(s_wohalf, n)
                nc.gpsimd.tensor_tensor(wo_lo[:], wo_raw[:], wo_hi[:], ALU.subtract).then_inc(s_wo, 1)

            split_wqkv(1)
            split_wo(1)
            with pool.Fori(0, G) as g:
                for b in range(FB):
                    pool.wait_ge(s_hidh, g * FB + b + 1)
                    nc.gpsimd.tensor_tensor(hid_lo[:, b, :], hid[:, b % 2, :], hid_hi[:, b, :],
                                            ALU.subtract).then_inc(s_hidl, 1)

            def head(h, last_head):
                for piece in range(VALS):
                    kb = slice(piece * 4, piece * 4 + 4)
                    v = v_sum[:, piece % 2, :].rearrange("p (k d) -> p k d", d=D)
                    pool.wait_ge(s_vsum, VALS * h + piece + 1)
                    nc.gpsimd.tensor_tensor(v_hi[:, kb, :], v, zeros_v, ALU.add).then_inc(s_vhi, 1)
                    pool.wait_ge(s_vhi, VALS * h + piece + 1)
                    nc.gpsimd.tensor_tensor(v_lo[:, kb, :], v, v_hi[:, kb, :], ALU.subtract).then_inc(s_vsplit, 1)
                for p in range(PAIRS):
                    if p == 1 and not last_head:
                        pool.wait_ge(s_val, VALS * h + 4)
                        split_wqkv(h + 2)
                    pool.wait_ge(s_osum, PAIRS * h + p + 1)
                    nc.gpsimd.tensor_tensor(o_hi[:], o_sum[:], zeros[:, 0, 0:2 * P], ALU.add).then_inc(s_ohi, 1)
                    pool.wait_ge(s_ohi, PAIRS * h + p + 1)
                    nc.gpsimd.tensor_tensor(o_lo[:], o_sum[:], o_hi[:], ALU.subtract).then_inc(s_osp, 1)
                if not last_head:
                    pool.wait_ge(s_y, PAIRS * h + 8)
                    split_wo(h + 2)

            with pool.Fori(0, H - 1) as h:
                head(h, False)
            head(H - 1, True)


def kernel(**inputs):
    import numpy as _np
    import concourse.bacc as _bacc
    from concourse.bass_utils import run_bass_kernel_spmd as _run

    nc = _bacc.Bacc("TRN2", target_bir_lowering=False, num_devices=1)
    wqkv = _np.asarray(inputs["L0_attn_Wqkv"]).reshape(3, H, D, C, P)
    arrays = {
        "x_dram": _np.asarray(inputs["L0_attn_x"]).reshape(S, DIM),
        "wqkv_dram": wqkv.transpose(1, 4, 3, 0, 2).reshape(H, P, C, 3 * D),
        "wo_dram": _np.asarray(inputs["L0_attn_Wout"]).T.reshape(H, P, DIM),
        "w1_dram": _np.asarray(inputs["L0_ffn_w1"]).T,
        "w2_dram": _np.asarray(inputs["L0_ffn_w2"]).T,
        "w3_dram": _np.asarray(inputs["L0_ffn_w3"]).T,
    }
    arrays = {k: _np.ascontiguousarray(v) for k, v in arrays.items()}
    args = [nc.dram_tensor(k, v.shape, F32, kind="ExternalInput").ap() for k, v in arrays.items()]
    args.append(nc.dram_tensor("out_dram", (S, DIM), F32, kind="ExternalOutput").ap())
    build(nc, *args)
    r = _run(nc, [arrays], core_ids=[0])
    return r.results[0]["out_dram"].reshape(1, S, DIM)
```

```python
import concourse.bass as bass
from concourse import mybir
from contextlib import ExitStack

F32 = mybir.dt.float32
F32R = mybir.dt.float32r
ALU = mybir.AluOpType
ACT = mybir.ActivationFunctionType
AX_X = mybir.AxisListType.X

P = 128
S = 2048
DIM = 256
H = 16
D = 128
FF = 704
C = DIM // P
T = S // P
PAIRS = T // 2
FB = -(-FF // P)
FR = FF - (FB - 1) * P
G = 4
CH = S // G
TG = CH // P
HALF = S // 2
KH = HALF // P
SCALE = float(D) ** -0.5
LN_EPS = 1e-5
Q_EPS = 1e-8

SCORES = EXPS = 2 * T
TRANS = PTH = PTL = 4 * T
PROJ = 8
VALS = 4
YACC = T


def build(nc, x_d, wqkv_d, wo_d, w1_d, w2_d, w3_d, out_d):
    ctx = ExitStack()
    with ctx:
        def sb(name, shape, dt=F32, where=ctx):
            return where.enter_context(nc.sbuf_tensor(name, shape, dt))

        def sem(name):
            return ctx.enter_context(nc.semaphore(name))

        y = sb("y", [P, T, DIM])
        xt_hi = sb("xt_hi", [P, C, S], F32R)
        xt_lo = sb("xt_lo", [P, C, S], F32R)
        with ExitStack() as first:
            xn = sb("xn", [P, T, DIM], where=first)
            below = sb("below", [P, FB * DIM], where=first)
            junk = sb("junk", [P, FB * DIM], where=first)
        k_hi = sb("k_hi", [P, S], F32R)
        k_lo = sb("k_lo", [P, S], F32R)
        q_hi = sb("q_hi", [P, S], F32R)
        q_lo = sb("q_lo", [P, S], F32R)
        v_hi = sb("v_hi", [P, T, D], F32R)
        v_lo = sb("v_lo", [P, T, D], F32R)
        wqkv_raw = sb("wqkv_raw", [P, C, 3 * D])
        wqkv = sb("wqkv", [P, C, 2, 3 * D], F32R)
        wo_raw = sb("wo_raw", [P, DIM])
        wo_hi = sb("wo_hi", [P, DIM], F32R)
        wo_lo = sb("wo_lo", [P, DIM], F32R)
        v_raw = sb("v_raw", [P, 2, 4, 2 * D])
        o_low = sb("o_low", [P, 2 * P])
        o_sum = sb("o_sum", [P, 2 * P])
        o_hi = sb("o_hi", [P, 2 * P], F32R)
        o_lo = sb("o_lo", [P, 2 * P], F32R)
        ident = sb("ident", [P, P])
        zeros = sb("zeros", [P, C, 3 * D])
        zeros_v = zeros[:].rearrange("p c e -> p (c e)")[:, 0:4 * D].rearrange("p (k d) -> p k d", d=D)
        row_max = sb("row_max", [P, T, 2])
        neg_max = sb("neg_max", [P, T])
        row_sum = sb("row_sum", [P, T, 2])
        denom = sb("denom", [P, T])
        inv_denom = sb("inv_denom", [P, T])

        with ExitStack() as early:
            w1_raw = sb("w1_raw", [P, C, FF], where=early)
            w2_raw = sb("w2_raw", [P, C, FF], where=early)
            w3_raw = sb("w3_raw", [P, FB, DIM], where=early)
            w1_q = sb("w1_q", [P, C, FB * P], F32R, early)
            w2_q = sb("w2_q", [P, C, FB * P], F32R, early)
            w3_q = sb("w3_q", [P, FB, DIM], F32R, early)
            ones = sb("ones", [P, P], where=early)
            abs_sum = sb("abs_sum", [P, 3], where=early)
            gamma = sb("gamma", [P, 3], where=early)
            half_gamma = sb("half_gamma", [P, 2, 3], where=early)
            stats = sb("stats", [P, T, 6], where=early)
            mean = sb("mean", [P, T], where=early)
            diff = sb("diff", [P, T], where=early)
            var_eps = sb("var_eps", [P, T], where=early)
            std = sb("std", [P, T], where=early)
            rstd = sb("rstd", [P, T], where=early)
            newton = sb("newton", [P, T], where=early)
            sig = sb("sig", [P, 2, CH], where=early)
            hid = sb("hid", [P, 2, CH], where=early)
            hid_hi = sb("hid_hi", [P, FB, CH], F32R, early)
            hid_lo = sb("hid_lo", [P, FB, CH], F32R, early)
        prob = sb("prob", [P, 2, S])
        pt = sb("pt", [P, 2, T, 4 * P], F32R)

        ps_s = ctx.enter_context(nc.psum_tensor("ps_s", [P, 4, 512], F32))
        ps_t = ctx.enter_context(nc.psum_tensor("ps_t", [P, 2, 512], F32))
        ps_o = ctx.enter_context(nc.psum_tensor("ps_o", [P, 2, 512], F32))

        s_x = [sem(f"x{g}_loaded") for g in range(G)]
        s_w = [sem("w1_loaded"), sem("w2_loaded"), sem("w3_loaded")]
        s_wqkv_in = sem("wqkv_loaded")
        s_wo_in = sem("wo_loaded")
        s_const = sem("constants_ready")
        s_pads = sem("pads_zeroed")
        s_w3_pad = sem("w3_pad_zeroed")
        s_abs = sem("abs_sums_ready")
        s_tot = sem("abs_totals_ready")
        s_gamma = sem("thresholds_step_done")
        s_below = sem("below_ready")
        s_wq = sem("quantised_weights_ready")
        s_ln = sem("layernorm_step_done")
        s_std = sem("std_ready")
        s_xn = sem("normalised_ready")
        s_xtr = sem("normalised_transposed")
        s_xth = sem("xt_high_ready")
        s_xtl = sem("xt_low_ready")
        s_up = sem("ffn_up_done")
        s_sig = sem("sigmoid_ready")
        s_hid = sem("hidden_ready")
        s_hidh = sem("hidden_high_ready")
        s_hidl = sem("hidden_low_ready")
        s_down = sem("ffn_down_done")
        s_wqkv = sem("wqkv_split")
        s_whalf = sem("wqkv_high_ready")
        s_wo = sem("wo_split")
        s_wohalf = sem("wo_high_ready")
        s_proj = sem("keys_queries_done")
        s_projh = sem("keys_queries_high_ready")
        s_projl = sem("keys_queries_low_ready")
        s_val = sem("values_done")
        s_vraw = sem("values_copied")
        s_vsum = sem("values_summed")
        s_vhi = sem("values_high_ready")
        s_vsplit = sem("values_split")
        s_scores = sem("logits_done")
        s_mx = sem("half_max_ready")
        s_nm = sem("neg_max_ready")
        s_exp = sem("exponentials_ready")
        s_tr = sem("transposes_done")
        s_pth = sem("pt_high_ready")
        s_ptl = sem("pt_low_ready")
        s_pv = sem("values_product_done")
        s_olow = sem("low_output_copied")
        s_osum = sem("output_summed")
        s_ohi = sem("output_high_ready")
        s_osp = sem("output_split")
        s_den = sem("denominator_ready")
        s_inv = sem("inverse_ready")
        s_y = sem("projection_done")
        s_yacc = sem("result_added")
        s_out = sem("result_stored")

        block = ctx.enter_context(nc.Block())

        @block.sync
        def _(sp):
            x_v = x_d.rearrange("(t p) c -> p t c", p=P)
            for g in range(G):
                sp.dma_start(y[:, g * TG:(g + 1) * TG, :], x_v[:, g * TG:(g + 1) * TG, :]).then_inc(s_x[g], 16)
            sp.dma_start(w1_raw[:], w1_d.rearrange("(c p) f -> p c f", p=P)).then_inc(s_w[0], 16)
            sp.dma_start(w2_raw[:], w2_d.rearrange("(c p) f -> p c f", p=P)).then_inc(s_w[1], 16)
            sp.dma_start(w3_raw[:, 0:FB - 1, :],
                         w3_d[0:(FB - 1) * P, :].rearrange("(b p) c -> p b c", p=P)).then_inc(s_w[2], 16)
            sp.dma_start(w3_raw[0:FR, FB - 1, :], w3_d[(FB - 1) * P:FF, :]).then_inc(s_w[2], 16)
            sp.dma_start(wqkv_raw[:], wqkv_d[0:1].rearrange("h p c e -> p (h c) e")).then_inc(s_wqkv_in, 16)
            sp.dma_start(wo_raw[:], wo_d[0:1].rearrange("h p c -> p (h c)")).then_inc(s_wo_in, 16)
            with sp.Fori(0, H - 1) as h:
                sp.wait_ge(s_wqkv, h + 1)
                sp.dma_start(wqkv_raw[:],
                             wqkv_d[bass.ds(h + 1, 1)].rearrange("h p c e -> p (h c) e")).then_inc(s_wqkv_in, 16)
                sp.wait_ge(s_wo, h + 1)
                sp.dma_start(wo_raw[:],
                             wo_d[bass.ds(h + 1, 1)].rearrange("h p c -> p (h c)")).then_inc(s_wo_in, 16)
            out_v = out_d.rearrange("(t p) c -> p t c", p=P)
            for p in range(PAIRS):
                sp.wait_ge(s_yacc, YACC * H + 2 * p + 2)
                sp.dma_start(out_v[:, 2 * p:2 * p + 2, :], y[:, 2 * p:2 * p + 2, :]).then_inc(s_out, 16)
            sp.wait_ge(s_out, 16 * PAIRS)

        @block.tensor
        def _(pe):
            def project(first, part, half):
                for bank in (2 * half, 2 * half + 1):
                    col = slice(bank * 512, bank * 512 + 512)
                    n = 0
                    for c in range(C):
                        for w, x in ((0, xt_hi), (0, xt_lo), (1, xt_hi)):
                            last = nc.tensor.matmul(ps_s[:, bank, :], wqkv[:, c, w, part * D:(part + 1) * D],
                                                    x[:, c, col], start=(n == 0), stop=(n == 3 * C - 1))
                            n += 1
                    last.then_inc(s_proj, 1)

            def values(banks, piece):
                for j in range(4):
                    kb = piece * 4 + j
                    dst = banks[:, j // 2, (j % 2) * 2 * D:(j % 2 + 1) * 2 * D]
                    for c in range(C):
                        nc.tensor.matmul(dst.rearrange("p (a d) -> p a d", d=D), xt_hi[:, c, kb * P:(kb + 1) * P],
                                         wqkv[:, c, :, 2 * D:3 * D], start=(c == 0), stop=(c == C - 1),
                                         skip_group_check=True)
                        last = nc.tensor.matmul(dst[:, 0:D], xt_lo[:, c, kb * P:(kb + 1) * P],
                                                wqkv[:, c, 0, 2 * D:3 * D], start=False, stop=(c == C - 1),
                                                skip_group_check=True)
                last.then_inc(s_val, 1)

            def logits(t, half):
                for bank in (2 * half, 2 * half + 1):
                    col = slice(bank * 512, bank * 512 + 512)
                    tile = slice(t * P, (t + 1) * P)
                    nc.tensor.matmul(ps_s[:, bank, :], q_hi[:, tile], k_hi[:, col], start=True, stop=False)
                    nc.tensor.matmul(ps_s[:, bank, :], q_hi[:, tile], k_lo[:, col], start=False, stop=False)
                    last = nc.tensor.matmul(ps_s[:, bank, :], q_lo[:, tile], k_hi[:, col], start=False, stop=True)
                last.then_inc(s_scores, 1)

            def transposes(h, t, half):
                pe.wait_ge(s_exp, EXPS * h + 2 * t + half + 1)
                for bank in (0, 1):
                    if 2 * t + half:
                        pe.wait_ge(s_ptl, PTL * h + 4 * t + 2 * half - 1 + bank)
                    for i in range(4):
                        kb = half * KH + 4 * bank + i
                        last = nc.tensor.transpose(ps_t[:, bank, i * P:(i + 1) * P],
                                                   prob[:, t % 2, kb * P:(kb + 1) * P], ident[:])
                    last.then_inc(s_tr, 1)

            def products(p, half):
                for i in range(KH):
                    kb = half * KH + i
                    nc.tensor.matmul(ps_o[:, p % 2, :], v_hi[:, kb, :], pt[:, p % 2, kb, :],
                                     start=(kb == 0), stop=(kb == T - 1), skip_group_check=True)
                    last = nc.tensor.matmul(ps_o[:, p % 2, 0:2 * P], v_lo[:, kb, :], pt[:, p % 2, kb, 0:2 * P],
                                            start=False, stop=(kb == T - 1), skip_group_check=True)
                if half:
                    last.then_inc(s_pv, 1)

            def out_projection(p):
                for j in range(2):
                    tile = slice(j * P, (j + 1) * P)
                    dst = ps_o[:, p % 2, j * DIM:(j + 1) * DIM]
                    nc.tensor.matmul(dst, o_hi[:, tile], wo_hi[:], start=True, stop=False)
                    nc.tensor.matmul(dst, o_hi[:, tile], wo_lo[:], start=False, stop=False)
                    last = nc.tensor.matmul(dst, o_lo[:, tile], wo_hi[:], start=False, stop=True)
                last.then_inc(s_y, 1)

            def transpose_x(g):
                pe.wait_ge(s_xn, g + 1)
                for c in range(C):
                    if g:
                        pe.wait_ge(s_xtl, C * (g - 1) + c + 1)
                    for j in range(TG):
                        last = nc.tensor.transpose(ps_t[:, c, j * P:(j + 1) * P],
                                                   xn[:, g * TG + j, c * P:(c + 1) * P], ident[:])
                    last.then_inc(s_xtr, 1)

            def ffn_up(g, b, first=False):
                if b >= 2:
                    pe.wait_ge(s_hid, g * FB + b - 1)
                for w, k in ((w1_q, 0), (w2_q, 1)):
                    if first and k:
                        pe.wait_ge(s_wq, 2)
                    n = 0
                    for c in range(C):
                        for x in (xt_hi, xt_lo):
                            last = nc.tensor.matmul(ps_s[:, 2 * (b % 2) + k, :], w[:, c, b * P:(b + 1) * P],
                                                    x[:, c, bass.ds(g * CH, CH)],
                                                    start=(n == 0), stop=(n == 2 * C - 1))
                            n += 1
                last.then_inc(s_up, 1)

            def ffn_down(g):
                for b in range(FB):
                    pe.wait_ge(s_hidl, g * FB + b + 1)
                    for j in range(TG):
                        dst = (ps_t if j < 2 else ps_o)[:, j % 2, 0:DIM]
                        nc.tensor.matmul(dst, hid_hi[:, b, j * P:(j + 1) * P], w3_q[:, b, :],
                                         start=(b == 0), stop=False)
                        last = nc.tensor.matmul(dst, hid_lo[:, b, j * P:(j + 1) * P], w3_q[:, b, :],
                                                start=False, stop=(b == FB - 1))
                last.then_inc(s_down, 1)

            pe.wait_ge(s_const, 1)
            pe.wait_ge(s_abs, 2)
            nc.tensor.matmul(ps_o[:, 0, 0:2], ones[:], abs_sum[:, 0:2], start=True, stop=True).then_inc(s_tot, 1)
            transpose_x(0)
            pe.wait_ge(s_abs, 3)
            nc.tensor.matmul(ps_o[:, 1, 0:1], ones[:], abs_sum[:, 2:3], start=True, stop=True).then_inc(s_tot, 1)
            pe.wait_ge(s_wq, 1)
            pe.wait_ge(s_xtl, C)
            for b in range(FB):
                ffn_up(0, b, b == 0)
                if b + 1 < G:
                    transpose_x(b + 1)
            pe.wait_ge(s_wq, 3)
            pe.wait_ge(s_xtl, C * G)
            ffn_down(0)
            with pe.Fori(1, G) as g:
                for b in range(FB):
                    ffn_up(g, b)
                pe.wait_ge(s_yacc, TG * g)
                ffn_down(g)
            pe.wait_ge(s_hid, G * FB)
            pe.wait_ge(s_wqkv, 1)
            for part in (1, 0):
                for half in (0, 1):
                    if part == 0:
                        pe.wait_ge(s_projl, 2 * half + 2)
                    project(0, part, half)
            pe.wait_ge(s_yacc, YACC)

            def head(h, last_head):
                for t in range(T):
                    for half in (0, 1):
                        if t == 0:
                            pe.wait_ge(s_projl, PROJ * h + 6 + 2 * half)
                        else:
                            pe.wait_ge(s_exp, EXPS * h + 2 * (t - 1) + half + 1)
                        logits(t, half)
                    if t == 0:
                        pe.wait_ge(s_wqkv, h + 1)
                        values(ps_t, 0)
                        pe.wait_ge(s_yacc, YACC * h + 16)
                        values(ps_o, 1)
                    if t >= 1:
                        if t == 1:
                            pe.wait_ge(s_vraw, VALS * h + 1)
                        transposes(h, t - 1, 0)
                    if t == 1:
                        pe.wait_ge(s_vraw, VALS * h + 2)
                        values(ps_o, 2)
                    if t == 2:
                        pe.wait_ge(s_vraw, VALS * h + 3)
                        values(ps_o, 3)
                    if t >= 3 and t % 2:
                        p = (t - 3) // 2
                        if p == 0:
                            pe.wait_ge(s_vraw, VALS * h + 4)
                            pe.wait_ge(s_vsplit, VALS * h + 2)
                        if p >= 2:
                            pe.wait_ge(s_yacc, YACC * h + 16 + 2 * (p - 1))
                        pe.wait_ge(s_ptl, PTL * h + 4 * (2 * p + 1) + 2)
                        products(p, 0)
                    if t >= 4 and t % 2 == 0:
                        p = (t - 4) // 2
                        if p == 0:
                            pe.wait_ge(s_vsplit, VALS * h + 4)
                        pe.wait_ge(s_ptl, PTL * h + 4 * (2 * p + 2))
                        products(p, 1)
                    if t >= 5 and t % 2:
                        p = (t - 5) // 2
                        if p == 0:
                            pe.wait_ge(s_wo, h + 1)
                        pe.wait_ge(s_osp, PAIRS * h + p + 1)
                        out_projection(p)
                    if t >= 1:
                        transposes(h, t - 1, 1)
                if not last_head:
                    pe.wait_ge(s_wqkv, h + 2)
                    for half in (0, 1):
                        pe.wait_ge(s_exp, EXPS * h + 2 * (T - 1) + half + 1)
                        project(h, 1, half)
                transposes(h, T - 1, 0)
                pe.wait_ge(s_ptl, PTL * h + 4 * 14)
                products(6, 1)
                transposes(h, T - 1, 1)
                pe.wait_ge(s_yacc, YACC * h + 16 + 2 * 6)
                products(7, 0)
                pe.wait_ge(s_osp, PAIRS * h + 7)
                out_projection(6)
                pe.wait_ge(s_ptl, PTL * h + 4 * T)
                products(7, 1)
                if not last_head:
                    for half in (0, 1):
                        pe.wait_ge(s_projl, PROJ * (h + 1) + 2 * half + 2)
                        project(h, 0, half)
                pe.wait_ge(s_osp, PAIRS * h + 8)
                out_projection(7)

            with pe.Fori(0, H - 1) as h:
                head(h, False)
            head(H - 1, True)

        @block.scalar
        def _(act):
            act.wait_ge(s_ln, 4)
            nc.scalar.activation(std[:], var_eps[:], ACT.Sqrt).then_inc(s_std, 1)

            def abs_sums(i, w):
                if i:
                    act.wait_ge(s_abs, i)
                n = w.shape[1] * w.shape[2]
                nc.scalar.activation(junk[:, 0:n], w[:].rearrange("p c f -> p (c f)"), ACT.Abs,
                                     accum_out=abs_sum[:, i:i + 1]).then_inc(s_abs, 1)

            def xt_high(g):
                for c in range(C):
                    act.wait_ge(s_xtr, C * g + c + 1)
                    nc.scalar.copy(xt_hi[:, c, g * CH:(g + 1) * CH], ps_t[:, c, :]).then_inc(s_xth, 1)

            def sigmoid(g, b):
                act.wait_ge(s_up, g * FB + b + 1)
                if b >= 2:
                    act.wait_ge(s_hid, g * FB + b - 1)
                nc.scalar.activation(sig[:, b % 2, :], ps_s[:, 2 * (b % 2), :], ACT.Sigmoid).then_inc(s_sig, 1)

            def hidden_high(g, b):
                act.wait_ge(s_hid, g * FB + b + 1)
                nc.scalar.copy(hid_hi[:, b, :], hid[:, b % 2, :]).then_inc(s_hidh, 1)

            act.wait_ge(s_w[0], 16)
            abs_sums(0, w1_raw)
            act.wait_ge(s_w[1], 16)
            abs_sums(1, w2_raw)
            xt_high(0)
            act.wait_ge(s_w[2], 32)
            act.wait_ge(s_w3_pad, 1)
            abs_sums(2, w3_raw)
            for b in range(FB + 1):
                if b < FB:
                    sigmoid(0, b)
                if b + 1 < G:
                    xt_high(b + 1)
                if b >= 1:
                    hidden_high(0, b - 1)
            with act.Fori(1, G) as g:
                for b in range(FB + 1):
                    if b < FB:
                        sigmoid(g, b)
                    if b >= 1:
                        hidden_high(g, b - 1)

            def proj_high(n, dst, bank):
                act.wait_ge(s_proj, n)
                nc.scalar.copy(dst[:, bank * 512:(bank + 1) * 512], ps_s[:, bank, :]).then_inc(s_projh, 1)

            def copy_values(h, banks, piece):
                act.wait_ge(s_val, VALS * h + piece + 1)
                if piece >= 2:
                    act.wait_ge(s_vsplit, VALS * h + piece - 1)
                nc.scalar.copy(v_raw[:, piece % 2].rearrange("p k n -> p (k n)"),
                               banks[:].rearrange("p b n -> p (b n)")).then_inc(s_vraw, 1)

            def pt_high(h, t, half):
                for bank in (0, 1):
                    kb = half * KH + 4 * bank
                    act.wait_ge(s_tr, TRANS * h + 4 * t + 2 * half + bank + 1)
                    nc.scalar.copy(pt[:, (t // 2) % 2, kb:kb + 4, (t % 2) * P:(t % 2 + 1) * P],
                                   ps_t[:, bank, :].rearrange("p (k q) -> p k q", q=P)).then_inc(s_pth, 1)

            def exponential(h, t, half):
                act.wait_ge(s_nm, T * h + t + 1)
                nc.scalar.activation(prob[:, t % 2, half * HALF:(half + 1) * HALF],
                                     ps_s[:, 2 * half:2 * half + 2, :].rearrange("p b n -> p (b n)"), ACT.Exp,
                                     bias=neg_max[:, t:t + 1], scale=SCALE,
                                     accum_out=row_sum[:, t, half:half + 1]).then_inc(s_exp, 1)

            def low_output(h, p):
                act.wait_ge(s_pv, PAIRS * h + p + 1)
                nc.scalar.copy(o_low[:], ps_o[:, p % 2, 2 * P:4 * P]).then_inc(s_olow, 1)

            for bank in range(4):
                proj_high(bank + 1, k_hi, bank)
            for bank in range(4):
                proj_high(bank + 5, q_hi, bank)

            def head(h, last_head):
                for t in range(T):
                    if t >= 5 and t % 2:
                        low_output(h, (t - 5) // 2)
                    if t >= 2:
                        pt_high(h, t - 2, 1)
                    if t in (2, 3):
                        copy_values(h, ps_o, t)
                    if t >= 1:
                        pt_high(h, t - 1, 0)
                    exponential(h, t, 0)
                    exponential(h, t, 1)
                    if t == 0:
                        copy_values(h, ps_t, 0)
                        copy_values(h, ps_o, 1)
                pt_high(h, T - 2, 1)
                if not last_head:
                    for bank in range(4):
                        proj_high(PROJ * (h + 1) + bank + 1, k_hi, bank)
                pt_high(h, T - 1, 0)
                low_output(h, 6)
                pt_high(h, T - 1, 1)
                low_output(h, 7)
                if not last_head:
                    for bank in range(4):
                        proj_high(PROJ * (h + 1) + bank + 5, q_hi, bank)

            with act.Fori(0, H - 1) as h:
                head(h, False)
            head(H - 1, True)

        @block.vector
        def _(dve):
            for t in range(T):
                if t % TG == 0:
                    dve.wait_ge(s_x[t // TG], 16)
                last = nc.vector.bn_stats(stats[:, t, :], y[:, t, :])
            last.then_inc(s_ln, 1)
            dve.wait_ge(s_ln, 1)
            nc.vector.tensor_tensor(mean[:], stats[:, :, 1], stats[:, :, 4], ALU.add)
            nc.vector.tensor_tensor(diff[:], stats[:, :, 1], stats[:, :, 4], ALU.subtract)
            nc.vector.tensor_tensor(var_eps[:], stats[:, :, 2], stats[:, :, 5], ALU.add).then_inc(s_ln, 1)
            dve.wait_ge(s_ln, 2)
            nc.vector.tensor_scalar(mean[:], mean[:], 0.5, None, ALU.mult)
            nc.vector.tensor_tensor(diff[:], diff[:], diff[:], ALU.mult)
            nc.vector.tensor_scalar(var_eps[:], var_eps[:], 1.0 / DIM, LN_EPS, ALU.mult, ALU.add).then_inc(s_ln, 1)
            dve.wait_ge(s_ln, 3)
            nc.vector.scalar_tensor_tensor(out=var_eps[:], in0=diff[:], scalar=0.25, in1=var_eps[:],
                                           op0=ALU.mult, op1=ALU.add).then_inc(s_ln, 1)
            dve.wait_ge(s_std, 1)
            nc.vector.reciprocal(rstd[:], std[:]).then_inc(s_ln, 1)
            dve.wait_ge(s_ln, 5)
            nc.vector.tensor_tensor(newton[:], rstd[:], rstd[:], ALU.mult).then_inc(s_ln, 1)
            dve.wait_ge(s_ln, 6)
            nc.vector.tensor_tensor(newton[:], newton[:], var_eps[:], ALU.mult).then_inc(s_ln, 1)
            dve.wait_ge(s_ln, 7)
            nc.vector.tensor_scalar(newton[:], newton[:], -0.5, 1.5, ALU.mult, ALU.add).then_inc(s_ln, 1)
            dve.wait_ge(s_ln, 8)
            nc.vector.tensor_tensor(rstd[:], rstd[:], newton[:], ALU.mult).then_inc(s_ln, 1)
            dve.wait_ge(s_ln, 9)

            def normalise(g):
                for t in range(g * TG, (g + 1) * TG):
                    last = nc.vector.tensor_scalar(xn[:, t, :], y[:, t, :], mean[:, t:t + 1], rstd[:, t:t + 1],
                                                   ALU.subtract, ALU.mult)
                last.then_inc(s_xn, 1)

            def xt_low(g):
                col = slice(g * CH, (g + 1) * CH)
                for c in range(C):
                    dve.wait_ge(s_xth, C * g + c + 1)
                    nc.vector.tensor_tensor(xt_lo[:, c, col], ps_t[:, c, :], xt_hi[:, c, col], ALU.subtract
                                            ).then_inc(s_xtl, 1)

            def thresholds(n, totals, cols):
                dve.wait_ge(s_tot, n)
                nc.vector.tensor_scalar(gamma[:, cols], totals, 1.0 / (FF * DIM), Q_EPS, ALU.mult, ALU.add
                                        ).then_inc(s_gamma, 1)
                dve.wait_ge(s_gamma, 3 * n - 2)
                nc.vector.tensor_scalar(half_gamma[:, 0, cols], gamma[:, cols], 0.5, None, ALU.mult
                                        ).then_inc(s_gamma, 1)
                nc.vector.tensor_scalar(half_gamma[:, 1, cols], gamma[:, cols], -0.5, None, ALU.mult
                                        ).then_inc(s_gamma, 1)

            def quantise(i, raw, q):
                n = raw.shape[1] * raw.shape[2]
                is_below = below[:, 0:n].rearrange("p (b c) -> p b c", b=raw.shape[1])
                if i:
                    dve.wait_ge(s_wq, i)
                nc.vector.tensor_scalar(is_below, raw[:], half_gamma[:, 1, i:i + 1], None, ALU.is_lt
                                        ).then_inc(s_below, 1)
                dve.wait_ge(s_below, i + 1)
                nc.vector.scalar_tensor_tensor(out=q, in0=raw[:], scalar=half_gamma[:, 0, i:i + 1], in1=is_below,
                                               op0=ALU.is_gt, op1=ALU.subtract).then_inc(s_wq, 1)

            normalise(0)
            thresholds(1, ps_o[:, 0, 0:2], slice(0, 2))
            dve.wait_ge(s_gamma, 3)
            quantise(0, w1_raw, w1_q[:, :, 0:FF])
            xt_low(0)
            quantise(1, w2_raw, w2_q[:, :, 0:FF])
            normalise(1)
            normalise(2)
            thresholds(2, ps_o[:, 1, 0:1], slice(2, 3))

            def hidden(g, b):
                dve.wait_ge(s_sig, g * FB + b + 1)
                if b >= 2:
                    dve.wait_ge(s_hidl, g * FB + b - 1)
                nc.vector.tensor_tensor(hid[:, b % 2, :], ps_s[:, 2 * (b % 2) + 1, :], sig[:, b % 2, :],
                                        ALU.mult).then_inc(s_hid, 1)

            def add_ffn(g):
                dve.wait_ge(s_down, g + 1)
                for j in range(TG):
                    tile = y[:, bass.ds(g * TG + j, 1), :].rearrange("p t c -> p (t c)")
                    nc.vector.tensor_tensor(tile, (ps_t if j < 2 else ps_o)[:, j % 2, 0:DIM], tile,
                                            ALU.add).then_inc(s_yacc, 1)

            for b in range(FB):
                hidden(0, b)
                if b + 1 < G:
                    xt_low(b + 1)
                if b == 0:
                    normalise(G - 1)
                if b == 3:
                    dve.wait_ge(s_gamma, 6)
                    quantise(2, w3_raw, w3_q[:])
            add_ffn(0)
            with dve.Fori(1, G) as g:
                for b in range(FB):
                    hidden(g, b)
                add_ffn(g)

            def proj_low(n, lo, hi, bank):
                col = slice(bank * 512, (bank + 1) * 512)
                dve.wait_ge(s_projh, n)
                nc.vector.tensor_tensor(lo[:, col], ps_s[:, bank, :], hi[:, col], ALU.subtract).then_inc(s_projl, 1)

            def pt_low(h, t, half):
                hi = (t % 2) * P
                lo = 2 * P + hi
                for bank in (0, 1):
                    kb = half * KH + 4 * bank
                    dve.wait_ge(s_pth, PTH * h + 4 * t + 2 * half + bank + 1)
                    nc.vector.tensor_tensor(pt[:, (t // 2) % 2, kb:kb + 4, lo:lo + P],
                                            ps_t[:, bank, :].rearrange("p (k q) -> p k q", q=P),
                                            pt[:, (t // 2) % 2, kb:kb + 4, hi:hi + P], ALU.subtract
                                            ).then_inc(s_ptl, 1)

            def maximum(h, t):
                for half in (0, 1):
                    dve.wait_ge(s_scores, SCORES * h + 2 * t + half + 1)
                    nc.vector.reduce_max(row_max[:, t, half:half + 1],
                                         ps_s[:, 2 * half:2 * half + 2, :].rearrange("p b n -> p (b n)"),
                                         AX_X).then_inc(s_mx, 1)
                dve.wait_ge(s_mx, 2 * T * h + 2 * t + 2)
                nc.vector.tensor_scalar(neg_max[:, t:t + 1], row_max[:, t, 0:1], row_max[:, t, 1:2], -SCALE,
                                        ALU.max, ALU.mult).then_inc(s_nm, 1)

            def output_sum(h, p):
                dve.wait_ge(s_olow, PAIRS * h + p + 1)
                nc.vector.tensor_tensor(o_sum[:], ps_o[:, p % 2, 0:2 * P], o_low[:], ALU.add).then_inc(s_osum, 1)
                dve.wait_ge(s_exp, EXPS * h + 4 * p + 4)
                nc.vector.tensor_tensor(denom[:, 2 * p:2 * p + 2], row_sum[:, 2 * p:2 * p + 2, 0],
                                        row_sum[:, 2 * p:2 * p + 2, 1], ALU.add).then_inc(s_den, 1)

            def inverse(h, p):
                dve.wait_ge(s_den, PAIRS * h + p + 1)
                nc.vector.reciprocal(inv_denom[:, 2 * p:2 * p + 2], denom[:, 2 * p:2 * p + 2]).then_inc(s_inv, 1)

            def result(h, p, j):
                t = 2 * p + j
                dve.wait_ge(s_inv, PAIRS * h + p + 1)
                dve.wait_ge(s_y, PAIRS * h + p + 1)
                nc.vector.scalar_tensor_tensor(out=y[:, t, :], in0=ps_o[:, p % 2, j * DIM:(j + 1) * DIM],
                                               scalar=inv_denom[:, t:t + 1], in1=y[:, t, :],
                                               op0=ALU.mult, op1=ALU.add).then_inc(s_yacc, 1)

            for bank in range(4):
                proj_low(bank + 1, k_lo, k_hi, bank)
            for bank in range(4):
                proj_low(bank + 5, q_lo, q_hi, bank)

            def head(h, last_head):
                for t in range(T):
                    if t >= 5 and t % 2:
                        output_sum(h, (t - 5) // 2)
                    if t >= 2:
                        pt_low(h, t - 2, 1)
                    maximum(h, t)
                    if t >= 1:
                        pt_low(h, t - 1, 0)
                    if t >= 5 and t % 2:
                        inverse(h, (t - 5) // 2)
                    if t >= 6 and t % 2 == 0:
                        result(h, (t - 6) // 2, 0)
                        result(h, (t - 6) // 2, 1)
                pt_low(h, T - 2, 1)
                result(h, 5, 0)
                result(h, 5, 1)
                if not last_head:
                    for bank in range(4):
                        proj_low(PROJ * (h + 1) + bank + 1, k_lo, k_hi, bank)
                pt_low(h, T - 1, 0)
                output_sum(h, 6)
                pt_low(h, T - 1, 1)
                inverse(h, 6)
                output_sum(h, 7)
                result(h, 6, 0)
                result(h, 6, 1)
                inverse(h, 7)
                if not last_head:
                    for bank in range(4):
                        proj_low(PROJ * (h + 1) + bank + 5, q_lo, q_hi, bank)
                result(h, 7, 0)
                result(h, 7, 1)

            with dve.Fori(0, H - 1) as h:
                head(h, False)
            head(H - 1, True)

        @block.gpsimd
        def _(pool):
            nc.gpsimd.memset(ident[:], 0.0).then_inc(s_pads, 1)
            nc.gpsimd.memset(w1_q[:, :, FF:FB * P].bitcast(F32), 0.0).then_inc(s_pads, 1)
            nc.gpsimd.memset(w2_q[:, :, FF:FB * P].bitcast(F32), 0.0).then_inc(s_pads, 1)
            pool.wait_ge(s_pads, 3)
            nc.gpsimd.memset(w3_raw[FR:P, FB - 1, :], 0.0).then_inc(s_w3_pad, 1)
            pool.wait_ge(s_w3_pad, 1)
            nc.gpsimd.memset(ones[:], 1.0).then_inc(s_pads, 1)
            nc.gpsimd.memset(zeros[:], 0.0).then_inc(s_pads, 1)
            pool.wait_ge(s_pads, 5)
            nc.gpsimd.affine_select(out=ident[:], in_=ident[:], compare_op=ALU.not_equal, fill=1.0, base=0,
                                    pattern=[[-1, P]], channel_multiplier=1).then_inc(s_const, 1)
            def split_wqkv(n):
                pool.wait_ge(s_wqkv_in, 16 * n)
                nc.gpsimd.tensor_tensor(wqkv[:, :, 0, :], wqkv_raw[:], zeros[:], ALU.add).then_inc(s_whalf, 1)
                pool.wait_ge(s_whalf, n)
                nc.gpsimd.tensor_tensor(wqkv[:, :, 1, :], wqkv_raw[:], wqkv[:, :, 0, :], ALU.subtract
                                        ).then_inc(s_wqkv, 1)

            def split_wo(n):
                pool.wait_ge(s_wo_in, 16 * n)
                nc.gpsimd.tensor_tensor(wo_hi[:], wo_raw[:], zeros[:, 0, 0:DIM], ALU.add).then_inc(s_wohalf, 1)
                pool.wait_ge(s_wohalf, n)
                nc.gpsimd.tensor_tensor(wo_lo[:], wo_raw[:], wo_hi[:], ALU.subtract).then_inc(s_wo, 1)

            split_wqkv(1)
            split_wo(1)
            with pool.Fori(0, G) as g:
                for b in range(FB):
                    pool.wait_ge(s_hidh, g * FB + b + 1)
                    nc.gpsimd.tensor_tensor(hid_lo[:, b, :], hid[:, b % 2, :], hid_hi[:, b, :],
                                            ALU.subtract).then_inc(s_hidl, 1)

            def head(h, last_head):
                for piece in range(VALS):
                    kb = slice(piece * 4, piece * 4 + 4)
                    v = v_raw[:, piece % 2, :, 0:D]
                    pool.wait_ge(s_vraw, VALS * h + piece + 1)
                    nc.gpsimd.tensor_tensor(v, v, v_raw[:, piece % 2, :, D:2 * D], ALU.add).then_inc(s_vsum, 1)
                    pool.wait_ge(s_vsum, VALS * h + piece + 1)
                    nc.gpsimd.tensor_tensor(v_hi[:, kb, :], v, zeros_v, ALU.add).then_inc(s_vhi, 1)
                    pool.wait_ge(s_vhi, VALS * h + piece + 1)
                    nc.gpsimd.tensor_tensor(v_lo[:, kb, :], v, v_hi[:, kb, :], ALU.subtract).then_inc(s_vsplit, 1)
                for p in range(PAIRS):
                    if p == 1 and not last_head:
                        pool.wait_ge(s_val, VALS * h + 4)
                        split_wqkv(h + 2)
                    pool.wait_ge(s_osum, PAIRS * h + p + 1)
                    nc.gpsimd.tensor_tensor(o_hi[:], o_sum[:], zeros[:, 0, 0:2 * P], ALU.add).then_inc(s_ohi, 1)
                    pool.wait_ge(s_ohi, PAIRS * h + p + 1)
                    nc.gpsimd.tensor_tensor(o_lo[:], o_sum[:], o_hi[:], ALU.subtract).then_inc(s_osp, 1)
                if not last_head:
                    pool.wait_ge(s_y, PAIRS * h + 8)
                    split_wo(h + 2)

            with pool.Fori(0, H - 1) as h:
                head(h, False)
            head(H - 1, True)


def kernel(**inputs):
    import numpy as _np
    import concourse.bacc as _bacc
    from concourse.bass_utils import run_bass_kernel_spmd as _run

    nc = _bacc.Bacc("TRN2", target_bir_lowering=False, num_devices=1)
    wqkv = _np.asarray(inputs["L0_attn_Wqkv"]).reshape(3, H, D, C, P)
    arrays = {
        "x_dram": _np.asarray(inputs["L0_attn_x"]).reshape(S, DIM),
        "wqkv_dram": wqkv.transpose(1, 4, 3, 0, 2).reshape(H, P, C, 3 * D),
        "wo_dram": _np.asarray(inputs["L0_attn_Wout"]).T.reshape(H, P, DIM),
        "w1_dram": _np.asarray(inputs["L0_ffn_w1"]).T,
        "w2_dram": _np.asarray(inputs["L0_ffn_w2"]).T,
        "w3_dram": _np.asarray(inputs["L0_ffn_w3"]).T,
    }
    arrays = {k: _np.ascontiguousarray(v) for k, v in arrays.items()}
    args = [nc.dram_tensor(k, v.shape, F32, kind="ExternalInput").ap() for k, v in arrays.items()]
    args.append(nc.dram_tensor("out_dram", (S, DIM), F32, kind="ExternalOutput").ap())
    build(nc, *args)
    r = _run(nc, [arrays], core_ids=[0])
    return r.results[0]["out_dram"].reshape(1, S, DIM)
```
